# Optimizing a Trainium2 kernel written in Bass

```python
import numpy as np
import jax
import jax.numpy as jnp

def _softmax(x, axis=-1):
    return jax.nn.softmax(x, axis=axis)

def _gelu(x):
    return jax.nn.gelu(x, approximate=True)

def _silu(x):
    return jax.nn.silu(x)

def _sigmoid(x):
    return jax.nn.sigmoid(x)

def _layernorm(x, axis=-1, eps=1e-05):
    m = jnp.mean(x, axis=axis, keepdims=True)
    v = jnp.var(x, axis=axis, keepdims=True)
    return (x - m) / jnp.sqrt(v + eps)

def _scatter_add(tgt, idx, src, axis=0):
    return tgt.at[idx].add(src)

def _segment_sum(src, seg, n):
    return jax.ops.segment_sum(src, seg, n)
kernel_name = 'mk_macaron_d1_jaxref_r8_179046'

def setup_inputs(seed: int=0):
    np.random.seed(seed)
    _w = jnp.asarray

    def _L0_attn_setup():
        import jax, jax.numpy as jnp
        import numpy as np
        EPS_FEAT = 1.0 + 0.0001
        EPS_DEN = 1e-06

        def _linear_attention(x, W_qkv, b_qkv, W_out, b_out, num_heads=16):
            B, L, D = x.shape
            H = num_heads
            E = D // H
            qkv = x @ W_qkv + b_qkv
            q, k, v = jnp.split(qkv, 3, axis=-1)
            q = q.reshape(B, L, H, E)
            k = k.reshape(B, L, H, E)
            v = v.reshape(B, L, H, E)
            q = jax.nn.elu(q * E ** (-0.5)) + EPS_FEAT
            k = jax.nn.elu(k) + EPS_FEAT
            qL = jnp.moveaxis(q, 1, 0)
            kL = jnp.moveaxis(k, 1, 0)
            vL = jnp.moveaxis(v, 1, 0)
            kv0 = jnp.zeros((B, H, E, E), dtype=x.dtype)
            ks0 = jnp.zeros((B, H, E), dtype=x.dtype)

            def step(carry, qkv_t):
                kv_s, k_s = carry
                q_t, k_t, v_t = qkv_t
                kv_s = kv_s + jnp.einsum('bhe,bhf->bhef', k_t, v_t)
                k_s = k_s + k_t
                num = jnp.einsum('bhe,bhef->bhf', q_t, kv_s)
                den = jnp.einsum('bhe,bhe->bh', q_t, k_s)[..., None] + EPS_DEN
                return ((kv_s, k_s), num / den)
            _, out = jax.lax.scan(step, (kv0, ks0), (qL, kL, vL))
            out = jnp.moveaxis(out, 0, 1).reshape(B, L, D)
            return out @ W_out + b_out
        key = jax.random.key(seed)
        k1, k2, k3 = jax.random.split(key, 3)
        B, L, D = (4, 512, 128)
        x = jax.random.normal(k1, (B, L, D), dtype=jnp.float32)
        W_qkv = jax.random.normal(k2, (D, 3 * D), dtype=jnp.float32) / np.sqrt(D)
        b_qkv = jnp.zeros((3 * D,), dtype=jnp.float32)
        W_out = jax.random.normal(k3, (D, D), dtype=jnp.float32) / np.sqrt(D)
        b_out = jnp.zeros((D,), dtype=jnp.float32)
        return {'x': x, 'W_qkv': W_qkv, 'b_qkv': b_qkv, 'W_out': W_out, 'b_out': b_out}
    _L0_attn_in = _L0_attn_setup()

    def _L0_ffn_setup():
        import jax, jax.numpy as jnp
        import numpy as np
        E = 64
        K = 6
        CAP = 64
        ROUTE_SCALE = 1.0
        key = jax.random.key(seed)
        ks = jax.random.split(key, 9)
        B, S, D, I = (2, 128, 128, 88)
        SI = 2 * I
        s = 0.02
        return {'x': jax.random.normal(ks[0], (B, S, D), jnp.float32), 'gate_w': jax.random.normal(ks[1], (E, D), jnp.float32) * s, 'gate_b': jnp.zeros((E,), jnp.float32), 'w1': jax.random.normal(ks[2], (E, I, D), jnp.float32) * s, 'w2': jax.random.normal(ks[3], (E, D, I), jnp.float32) * s, 'w3': jax.random.normal(ks[4], (E, I, D), jnp.float32) * s, 'ws1': jax.random.normal(ks[5], (SI, D), jnp.float32) * s, 'ws2': jax.random.normal(ks[6], (D, SI), jnp.float32) * s, 'ws3': jax.random.normal(ks[7], (SI, D), jnp.float32) * s}
    _L0_ffn_in = _L0_ffn_setup()
    _d = {'L0_attn_x': _L0_attn_in['x'], 'L0_attn_W_qkv': _L0_attn_in['W_qkv'], 'L0_attn_b_qkv': _L0_attn_in['b_qkv'], 'L0_attn_W_out': _L0_attn_in['W_out'], 'L0_attn_b_out': _L0_attn_in['b_out'], 'L0_ffn_gate_w': _L0_ffn_in['gate_w'], 'L0_ffn_gate_b': _L0_ffn_in['gate_b'], 'L0_ffn_w1': _L0_ffn_in['w1'], 'L0_ffn_w2': _L0_ffn_in['w2'], 'L0_ffn_w3': _L0_ffn_in['w3'], 'L0_ffn_ws1': _L0_ffn_in['ws1'], 'L0_ffn_ws2': _L0_ffn_in['ws2'], 'L0_ffn_ws3': _L0_ffn_in['ws3']}
    _x0 = _d['L0_attn_x']
    _d['L0_attn_x'] = jax.random.normal(jax.random.fold_in(jax.random.key(seed), 1), (8, 512, 128), dtype=_x0.dtype)
    del _x0
    return _d

def reference(L0_attn_x, L0_attn_W_qkv, L0_attn_b_qkv, L0_attn_W_out, L0_attn_b_out, L0_ffn_gate_w, L0_ffn_gate_b, L0_ffn_w1, L0_ffn_w2, L0_ffn_w3, L0_ffn_ws1, L0_ffn_ws2, L0_ffn_ws3):

    def _L0_attn_ref(x, W_qkv, b_qkv, W_out, b_out):
        import jax, jax.numpy as jnp
        import numpy as np
        EPS_FEAT = 1.0 + 0.0001
        EPS_DEN = 1e-06

        def _linear_attention(x, W_qkv, b_qkv, W_out, b_out, num_heads=16):
            B, L, D = x.shape
            H = num_heads
            E = D // H
            qkv = x @ W_qkv + b_qkv
            q, k, v = jnp.split(qkv, 3, axis=-1)
            q = q.reshape(B, L, H, E)
            k = k.reshape(B, L, H, E)
            v = v.reshape(B, L, H, E)
            q = jax.nn.elu(q * E ** (-0.5)) + EPS_FEAT
            k = jax.nn.elu(k) + EPS_FEAT
            qL = jnp.moveaxis(q, 1, 0)
            kL = jnp.moveaxis(k, 1, 0)
            vL = jnp.moveaxis(v, 1, 0)
            kv0 = jnp.zeros((B, H, E, E), dtype=x.dtype)
            ks0 = jnp.zeros((B, H, E), dtype=x.dtype)

            def step(carry, qkv_t):
                kv_s, k_s = carry
                q_t, k_t, v_t = qkv_t
                kv_s = kv_s + jnp.einsum('bhe,bhf->bhef', k_t, v_t)
                k_s = k_s + k_t
                num = jnp.einsum('bhe,bhef->bhf', q_t, kv_s)
                den = jnp.einsum('bhe,bhe->bh', q_t, k_s)[..., None] + EPS_DEN
                return ((kv_s, k_s), num / den)
            _, out = jax.lax.scan(step, (kv0, ks0), (qL, kL, vL))
            out = jnp.moveaxis(out, 0, 1).reshape(B, L, D)
            return out @ W_out + b_out
        return _linear_attention(x, W_qkv, b_qkv, W_out, b_out)

    def _L0_ffn_ref(x, gate_w, gate_b, w1, w2, w3, ws1, ws2, ws3):
        import jax, jax.numpy as jnp
        import numpy as np
        E = 64
        K = 6
        CAP = 64
        ROUTE_SCALE = 1.0
        shape = x.shape
        D = shape[-1]
        xf = x.reshape(-1, D)
        T = xf.shape[0]
        scores = jax.nn.softmax(xf @ gate_w.T, axis=-1)
        _, idx = jax.lax.top_k(scores + gate_b, K)
        weights = jnp.take_along_axis(scores, idx, axis=1) * ROUTE_SCALE
        flat_e = idx.reshape(-1)
        order = jnp.argsort(flat_e)
        se = flat_e[order]
        counts = jnp.bincount(flat_e, length=E)
        starts = jnp.cumsum(counts) - counts
        pos = jnp.arange(T * K) - starts[se]
        tok = order // K
        xb = jnp.zeros((E, CAP, D), xf.dtype).at[se, pos].set(xf[tok], mode='drop')
        h = jax.nn.silu(jnp.einsum('ecd,eid->eci', xb, w1)) * jnp.einsum('ecd,eid->eci', xb, w3)
        yb = jnp.einsum('eci,edi->ecd', h, w2)
        valid = (pos < CAP).astype(xf.dtype)
        contrib = yb[se, jnp.minimum(pos, CAP - 1)]
        wf = weights.reshape(-1)[order] * valid
        y = jnp.zeros_like(xf).at[tok].add(contrib * wf[:, None])
        z = jax.nn.silu(xf @ ws1.T) * (xf @ ws3.T) @ ws2.T
        return (y + z).reshape(shape)
    x = L0_attn_x
    x = x + 0.5 * _L0_ffn_ref(_layernorm(x, axis=-1), L0_ffn_gate_w, L0_ffn_gate_b, L0_ffn_w1, L0_ffn_w2, L0_ffn_w3, L0_ffn_ws1, L0_ffn_ws2, L0_ffn_ws3)
    x = x + _L0_attn_ref(_layernorm(x, axis=-1), L0_attn_W_qkv, L0_attn_b_qkv, L0_attn_W_out, L0_attn_b_out)
    x = x + 0.5 * _L0_ffn_ref(_layernorm(x, axis=-1), L0_ffn_gate_w, L0_ffn_gate_b, L0_ffn_w1, L0_ffn_w2, L0_ffn_w3, L0_ffn_ws1, L0_ffn_ws2, L0_ffn_ws3)
    return x

_drawn_inputs = setup_inputs


def setup_inputs(seed=0):
    import zlib

    import numpy as np

    out = dict(_drawn_inputs(seed))
    spreads = {'L0_attn_b_qkv': (0.0, 0.1), 'L0_attn_b_out': (0.0, 0.1), 'L0_ffn_gate_b': (0.0, 0.8)}
    factors = {'L0_ffn_gate_w': 8.0,
     'L0_ffn_w1': 8.0,
     'L0_ffn_w2': 8.0,
     'L0_ffn_w3': 8.0,
     'L0_ffn_ws1': 8.0,
     'L0_ffn_ws2': 8.0,
     'L0_ffn_ws3': 8.0}
    for name, (base, spread) in spreads.items():
        noise = np.random.default_rng([zlib.crc32(name.encode()), seed]).standard_normal(out[name].shape)
        drawn = base * np.exp(spread * noise) if base else spread * noise
        out[name] = jnp.asarray(drawn.astype(out[name].dtype))
    for name, factor in factors.items():
        out[name] = (out[name] * factor).astype(out[name].dtype)
    return out
```

```python
from contextlib import ExitStack

import concourse.bass as bass
from concourse import mybir

ALU = mybir.AluOpType
ACT = mybir.ActivationFunctionType
AX = mybir.AxisListType.X
F32 = mybir.dt.float32
BF16 = mybir.dt.bfloat16
I32 = mybir.dt.int32

P = 128
TOPK = 6
CAP = 64
LN_EPS = 1e-5
FEAT_EPS = 1e-4
DEN_EPS = 1e-6
HEADS = 16
CHUNK = 32
NONE = -32768.0


def macaron_kernel(nc, x, w_qkv, b_qkv, w_out, b_out, gate_wT, gate_b, w1T, w2T, w3T, ws1T, ws2T, ws3T, out):
    B, L, D = x.shape
    T = B * L
    NI = T // P
    NE = gate_wT.shape[1]
    I = w1T.shape[2]
    NS = NE * CAP // P
    E = D // HEADS
    VW = HEADS * (E + 1)
    HV = VW // 2
    NQ = L // P
    NC = P // CHUNK
    RW = 2 * NI + 1
    PER = 7
    NG = 4
    GI = NI // NG
    NSH = NI // 4
    EARLY = 6
    BASE_AFTER = 4
    QS = float(E) ** -0.5
    STATES = ((0, 2), (6, 7))

    ctx = ExitStack()
    with ctx:
        def sb(name, shape, dt=F32):
            return ctx.enter_context(nc.sbuf_tensor(name, shape, dt))

        def sem(name):
            return ctx.enter_context(nc.semaphore(name))

        rows_d = nc.dram_tensor("rows_d", (T, D), F32, kind="Internal").ap()
        planes_d = [nc.dram_tensor(f"planes{f}_d", (4 * T, D), F32, kind="Internal").ap() for f in range(2)]
        attn_d = nc.dram_tensor("attn_d", (T, D), F32, kind="Internal").ap()

        X = sb("X", [P, NI, D])
        A = sb("A", [P, NI, D])
        XT = sb("XT", [P, T])
        Bb = sb("Bb", [P, NE * RW])
        Cb = sb("Cb", [P, 2 * NI * (NE + 2)])
        Eb = sb("Eb", [P, NE * NI])
        w1s = sb("w1s", [P, NE, I])
        w3s = sb("w3s", [P, NE, I])
        w2s = sb("w2s", [I, NE, D])
        ring = sb("ring", [P, 2 * (P + I + I + P)])
        ident = sb("ident", [P, P])
        before = sb("before", [P, P])
        causal = sb("causal", [P, CHUNK])
        own = sb("own", [P, VW])
        chm = sb("chm", [P, NC])
        hm = sb("hm", [P, 4])
        col_i = sb("col_i", [P, NI])
        c_of_p = sb("c_of_p", [P, 1])
        tok0 = sb("tok0", [P, 1])
        plane0 = sb("plane0", [P, 1])
        gate_s = sb("gate_s", [P, NE])
        gateb = sb("gateb", [P, NE])
        ws1s = sb("ws1s", [P, 2 * I])
        ws3s = sb("ws3s", [P, 2 * I])
        ws2s = sb("ws2s", [I, 2, D])
        wqkv = sb("wqkv", [P, 3 * D])
        wout = sb("wout", [P, D])
        bq = sb("bq", [P, 3])
        bv = sb("bv", [P, D])
        bo = sb("bo", [P, D])
        st = sb("st", [P, 8, NI])
        top8 = sb("top8", [P, NI, 8])
        st2 = sb("st2", [P, 6, NE])
        sl = sb("sl", [P, 3, NS])
        tok_i = sb("tok_i", [P, NS], I32)
        put_i = sb("put_i", [P, NS], I32)
        eps = sb("eps", [P, 1])
        zeros = sb("zeros", [P, 4 * D])
        PL = sb("PL", [P, NI * D])
        slot_ce = sb("slot_ce", [P, CAP, NE], BF16)
        bnd = sb("bnd", [P, 2, NE], BF16)
        bn = sb("bn", [P, NI, 6])
        mv = sb("mv", [P, NI, 2])

        A_flat = A[:, :, :].rearrange("p i d -> p (i d)")
        R = Bb[:, :].rearrange("p (e r) -> p e r", e=NE)
        Y = Bb[:, 0:NS * D].rearrange("p (s d) -> p s d", s=NS)
        BI = Cb[:, 0:NI * (NE + 2)].rearrange("p (i e) -> p i e", i=NI)
        RP = Cb[:, NI * (NE + 2):2 * NI * (NE + 2)].rearrange("p (i e) -> p i e", i=NI)
        OH = Cb[:, 0:NE * CAP].rearrange("p (e c) -> p e c", e=NE)
        HE = NE // 2
        GE, LT = (A_flat[:, 2048 + 1024 * k:3072 + 1024 * k].bitcast(BF16).rearrange("p (c e) -> p c e", c=CAP)
                  for k in range(2))
        EX = Eb[:, :].rearrange("p (i e) -> p i e", i=NI)
        M = Eb[:, :].rearrange("p (e i) -> p e i", e=NE)
        CUM = A_flat[:, 0:NE * NI].rearrange("p (e i) -> p e i", e=NE)
        LE = A_flat[:, 0:NS * NI].rearrange("p (s i) -> p s i", s=NS)
        G = A_flat[:, NS * NI:2 * NS * NI].rearrange("p (s i) -> p s i", s=NS)
        XBT = [ring[:, k * P:(k + 1) * P] for k in range(2)]
        o = 2 * P
        SG = [ring[:, o + k * I:o + (k + 1) * I] for k in range(2)]
        o += 2 * I
        GA = [ring[:, o + k * I:o + (k + 1) * I] for k in range(2)]
        o += 2 * I
        GT = [ring[0:I, o + k * P:o + (k + 1) * P] for k in range(2)]

        SH, H3, HS0, HS1 = (PL[0:I, 512 * k:512 * k + 512] for k in range(4))
        HS = (HS0, HS1)
        ZB = PL[:, 2048:2560]

        PR = A_flat[:, 0:4 * L]
        Q4 = A_flat[:, 4 * L:8 * L].rearrange("p (j t) -> p j t", j=4)
        VX = Bb[:, 0:NQ * NC * VW].rearrange("p (q h c f) -> p q h c f", q=NQ, h=HEADS, c=NC)
        o = NQ * NC * VW
        HTB, KT, QT0 = (Bb[:, o + k * L:o + (k + 1) * L] for k in range(3))
        SW = Cb[:, 0:NQ * NC * VW].rearrange("p (q c v) -> p q c v", q=NQ, c=NC)
        SB = Cb[:, o:o + NQ * VW].rearrange("p (q v) -> p q v", q=NQ)
        o += NQ * VW
        VN0 = Cb[:, o:o + NQ * VW]
        o += NQ * VW
        KN = Cb[:, o:o + L].rearrange("p (q k) -> p q k", q=NQ)
        EQ, RQ, AT, OO = (Eb[:, k * L:(k + 1) * L] for k in range(4))
        spare = w3s[:, :, :].rearrange("p e i -> p (e i)")
        QT1, EK, RK = (spare[:, k * L:(k + 1) * L] for k in range(3))
        QT = (QT0, QT1)
        VN = [v.rearrange("p (q h f) -> p q h f", q=NQ, h=HEADS) for v in (VN0, spare[:, 3 * L:3 * L + NQ * VW])]
        AN = ring[:, 0:L].rearrange("p (c k) -> p c k", c=NC)

        bank = [ctx.enter_context(nc.psum_tensor(f"bank{k}", [P, 512], F32)) for k in range(8)]

        part_in = [sem(f"part_in{g}") for g in range(NG)]
        small_in = sem("small_in")
        stats_ready = sem("stats_ready")
        mult_done = sem("mult_done")
        sh_read = sem("sh_read")
        sh_copied = sem("sh_copied")
        z_read = sem("z_read")
        x_free = sem("x_free")
        group_ready = sem("group_ready")
        w_in = sem("w_in")
        zero_set = sem("zero_set")
        planes_zero = sem("planes_zero")
        const_step = sem("const_step")
        const_done = sem("const_done")
        dve_step = sem("dve_step")
        std_ready = sem("std_ready")
        normed = sem("normed")
        xT_ps = sem("xT_ps")
        xT_sb = sem("xT_sb")
        rows_out = sem("rows_out")
        logits_ps = sem("logits_ps")
        shifted = sem("shifted")
        exp_done = sem("exp_done")
        totals = sem("totals")
        base_ps = sem("base_ps")
        table_ready = sem("table_ready")
        look_ps = sem("look_ps")
        slots_ready = sem("slots_ready")
        gathered = [sem(f"gathered{k}") for k in range(8)]
        xbT_ps = sem("xbT_ps")
        xbT_sb = sem("xbT_sb")
        h_ps = sem("h_ps")
        silu_done = sem("silu_done")
        gated = sem("gated")
        gT_ps = sem("gT_ps")
        gT_sb = sem("gT_sb")
        y_ps = sem("y_ps")
        y_sb = sem("y_sb")
        added = [sem(f"added{k}") for k in range(2)]
        sh_ps = sem("sh_ps")
        sh_gated = sem("sh_gated")
        z_ps = sem("z_ps")
        z_added = sem("z_added")
        out_done = sem("out_done")
        PRIMED = 1
        hTb_sb = sem("hTb_sb")
        qT_ps = sem("qT_ps")
        kT_ps = sem("kT_ps")
        v_ps = sem("v_ps")
        bq_scaled = sem("bq_scaled")
        q_read = sem("q_read")
        k_read = sem("k_read")
        phi_step = sem("phi_step")
        q_ready = sem("q_ready")
        k_ready = sem("k_ready")
        q4_ready = sem("q4_ready")
        v_ready = sem("v_ready")
        vx_ready = sem("vx_ready")
        kn_ps = sem("kn_ps")
        kn_sb = sem("kn_sb")
        sc_ps = sem("sc_ps")
        sc_sb = sem("sc_sb")
        kv_ps = sem("kv_ps")
        kv_sb = sem("kv_sb")
        sb_ready = sem("sb_ready")
        o_ps = sem("o_ps")
        o_step = sem("o_step")
        an_ready = sem("an_ready")
        anT_ps = sem("anT_ps")
        anT_sb = sem("anT_sb")
        pr_ps = sem("pr_ps")
        oo_ready = sem("oo_ready")
        attn_out = sem("attn_out")
        oo_stored = sem("oo_stored")
        attn_in = sem("attn_in")

        x_blk = x.rearrange("b l d -> (b l) d").rearrange("(p i) d -> p i d", p=P)
        out_blk = out.rearrange("b l d -> (b l) d").rearrange("(p i) d -> p i d", p=P)
        rows_blk = rows_d.rearrange("(p i) d -> p i d", p=P)
        PLANES = (A_flat, PL[:, :], Cb[:, 0:T], Bb[:, 0:T])
        N_SMALL = 12

        def shared_banks(g, k):
            return (0, 1) if k == 0 or g >= EARLY else (4, 5)

        block = ctx.enter_context(nc.Block())

        @block.sync
        def _(sp):
            for g in range(NG):
                sp.dma_start(X[:, GI * g:GI * g + GI, :], x_blk[:, GI * g:GI * g + GI, :]).then_inc(part_in[g], 16)
            sp.dma_start(gate_s[:, :], gate_wT).then_inc(small_in, 16)
            sp.dma_start(gateb[:, :], gate_b.rearrange("(a e) -> a e", a=1).broadcast_to([P, NE])).then_inc(small_in, 16)
            sp.dma_start(ws1s[:, :], ws1T).then_inc(small_in, 16)
            sp.dma_start(ws3s[:, :], ws3T).then_inc(small_in, 16)
            sp.dma_start(ws2s[:, :, :], ws2T).then_inc(small_in, 16)
            sp.dma_start(wqkv[:, :], w_qkv).then_inc(small_in, 16)
            sp.dma_start(wout[:, :], w_out).then_inc(small_in, 16)
            sp.dma_start(bq[:, 0:1], b_qkv[0:D].rearrange("(p a) -> p a", a=1)).then_inc(small_in, 16)
            sp.dma_start(bq[:, 1:2], b_qkv[D:2 * D].rearrange("(p a) -> p a", a=1)).then_inc(small_in, 16)
            sp.dma_start(bq[:, 2:3], b_qkv[0:D].rearrange("(p a) -> p a", a=1)).then_inc(small_in, 16)
            sp.dma_start(bv[:, :], b_qkv[2 * D:3 * D].rearrange("(a e) -> a e", a=1).broadcast_to([P, D])).then_inc(small_in, 16)
            sp.dma_start(bo[:, :], b_out.rearrange("(a e) -> a e", a=1).broadcast_to([P, D])).then_inc(small_in, 16)
            def clear_planes(f):
                for k in range(4):
                    dst = planes_d[f][k * T:(k + 1) * T, :].rearrange("(p a i) d -> p a (i d)", p=P, i=4)
                    sp.dma_start(dst, zeros[:, :].unsqueeze(1).broadcast_to([P, NI // 4, 4 * D])).then_inc(planes_zero, 16)

            sp.wait_ge(zero_set, 1)
            clear_planes(0)

            for f in range(2):
                for g in range(NG):
                    sp.wait_ge(normed, NG * 2 * f + g + 1)
                    sp.dma_start(rows_blk[:, GI * g:GI * g + GI, :], A[:, GI * g:GI * g + GI, :]).then_inc(rows_out, 16)
                if f == 0:
                    for dst, src in ((w1s, w1T), (w3s, w3T), (w2s, w2T)):
                        sp.dma_start(dst[:, :, :], src).then_inc(w_in, 16)
                for k in range(2):
                    sp.wait_ge(added[k], 16 * (NS // 2) * (f + 1))
                sp.wait_ge(z_added, NSH * (f + 1))
                for g in range(NG):
                    cols = slice(g * GI * D, (g + 1) * GI * D)
                    for k, buf in enumerate(PLANES):
                        src = planes_d[f][k * T:(k + 1) * T, :].rearrange("(p i) d -> p (i d)", p=P)
                        sp.dma_start(buf[:, cols], src[:, cols]).then_inc(part_in[g], 16)
                if f == 0:
                    clear_planes(1)
                    sp.sem_inc(oo_stored, PRIMED)
                    for b in range(B):
                        sp.wait_ge(oo_ready, PRIMED + b + 1)
                        for q in range(NQ):
                            sp.dma_start(attn_d[b * L + q * P:b * L + (q + 1) * P, :].rearrange("(c t) d -> t c d", t=CHUNK),
                                         OO[32 * q:32 * q + 32, :].rearrange("p (c d) -> p c d", c=NC)).then_inc(attn_out, 16)
                        sp.wait_ge(attn_out, 16 * NQ * (b + 1))
                        sp.sem_inc(oo_stored, 1)
                        rows = slice(P // B * b, P // B * (b + 1))
                        sp.wait_ge(group_ready, NG)
                        sp.dma_start(PL[rows, :], attn_d[b * L:(b + 1) * L, :].rearrange("(p i) d -> p (i d)", p=P // B))\
                            .then_inc(attn_in, 16)
                    sp.dma_start(w3s[:, :, :], w3T).then_inc(w_in, 16)
            for g in range(NG):
                sp.wait_ge(group_ready, NG + g + 1)
                sp.dma_start(out_blk[:, GI * g:GI * g + GI, :], X[:, GI * g:GI * g + GI, :]).then_inc(out_done, 16)
            sp.wait_ge(out_done, 16 * NG)
            sp.wait_ge(planes_zero, 16 * 8)

        @block.gpsimd
        def _(pool):
            made = [0]

            def then(ins):
                made[0] += 1
                ins.then_inc(const_step, 1)
                pool.wait_ge(const_step, made[0])

            def keep(t, op, base, pattern, per_partition, fill):
                then(pool.affine_select(out=t, in_=t, compare_op=op, fill=fill, base=base, pattern=pattern,
                                        channel_multiplier=per_partition))

            def count(t, base, pattern, per_partition):
                then(pool.iota(t, pattern=pattern, base=base, channel_multiplier=per_partition,
                               allow_small_or_imprecise_dtypes=True))

            then(pool.memset(eps[:, :], LN_EPS))
            then(pool.memset(ident[:, :], 0.0))
            keep(ident[:, :], ALU.not_equal, 0, [[-1, P]], 1, 1.0)
            then(pool.memset(before[:, :], 1.0))
            keep(before[:, :], ALU.is_gt, 0, [[1, P]], -1, 0.0)
            then(pool.memset(causal[:, :], 1.0))
            for c in range(NC):
                keep(causal[CHUNK * c:CHUNK * c + CHUNK, :], ALU.is_ge, 0, [[1, CHUNK]], -1, 0.0)
            then(pool.memset(own[:, :], 1.0))
            ov = own[:, :].rearrange("p (h f) -> p h f", h=HEADS)
            keep(ov, ALU.is_ge, 0, [[-E, HEADS], [0, E + 1]], 1, 0.0)
            keep(ov, ALU.is_ge, E - 1, [[E, HEADS], [0, E + 1]], -1, 0.0)
            then(pool.memset(chm[:, :], 1.0))
            keep(chm[:, :], ALU.is_ge, 0, [[-CHUNK, NC]], 1, 0.0)
            keep(chm[:, :], ALU.is_ge, CHUNK - 1, [[CHUNK, NC]], -1, 0.0)
            own3 = own[:, :].rearrange("p (g j f) -> p j g f", g=4, j=4)
            then(pool.tensor_tensor(out=hm[:, :], in0=own3[:, :, 0, 0], in1=own3[:, :, 1, 0], op=ALU.add))
            for k in (2, 3):
                then(pool.tensor_tensor(out=hm[:, :], in0=hm[:, :], in1=own3[:, :, k, 0], op=ALU.add))
            count(col_i[:, :], 0, [[1, NI]], 0)
            for k in range(2):
                count(c_of_p[k * CAP:(k + 1) * CAP, :], 0, [[0, 1]], 1)
                then(pool.memset(plane0[k * CAP:(k + 1) * CAP, :], float(k * T)))
            count(tok0[:, :], int(NONE), [[0, 1]], NI)
            count(slot_ce[:, :, :], 0, [[1, CAP], [0, NE]], 0)
            pool.memset(st2[:, 5, :], 0.0).then_inc(const_done, 1)

            for f in range(2):
                def shared(g):
                    for k in range(2):
                        n = (f * NSH + g) * 2 + k
                        pool.wait_ge(sh_copied, 2 * n + 2)
                        if g:
                            pool.wait_ge(z_ps, f * NSH + g)
                        pool.tensor_tensor(out=HS[k], in0=SH, in1=H3, op=ALU.mult).then_inc(sh_gated, 1)
                    pool.wait_ge(z_read, f * NSH + g + 1)
                    xs = X[:, 4 * g:4 * g + 4, :].rearrange("p i d -> p (i d)")
                    pool.tensor_tensor(out=xs, in0=xs, in1=ZB, op=ALU.add).then_inc(z_added, 1)

                pool.wait_ge(normed, NG * (2 * f + 1))
                for g in range(EARLY):
                    shared(g)
                pool.wait_ge(slots_ready, f + 1)
                pool.wait_ge(rows_out, 16 * NG * (f + 1))
                pool.wait_ge(planes_zero, 16 * 4 * (f + 1))

                def add(s):
                    pool.wait_ge(y_sb, f * NS + s + 1)
                    n = f * (NS // 2) + s // 2
                    if n:
                        pool.wait_ge(added[s % 2], 16 * n)
                    pool.indirect_dma_start(out=planes_d[f], in_=Y[:, s, :], in_offset=None,
                                            out_offset=bass.IndirectOffsetOnAxis(ap=put_i[:, s:s + 1], axis=0),
                                            bounds_check=4 * T - 1, oob_is_err=False,
                                            compute_op=ALU.add).then_inc(added[s % 2], 16)

                LAG = 6
                for s in range(NS + LAG):
                    if s < NS:
                        n = f * (NS // 8) + s // 8
                        if n:
                            pool.wait_ge(gathered[s % 8], 16 * n)
                        pool.indirect_dma_start(out=A[:, s, :], out_offset=None, in_=rows_d,
                                                in_offset=bass.IndirectOffsetOnAxis(ap=tok_i[:, s:s + 1], axis=0),
                                                bounds_check=T - 1, oob_is_err=False).then_inc(gathered[s % 8], 16)
                    if s >= LAG:
                        add(s - LAG)
                    if s in (2, 3):
                        shared(EARLY + s - 2)
                if f == 0:
                    pool.wait_ge(group_ready, NG)
                    pool.sem_inc(vx_ready, PRIMED)

                    def block_diagonal(b, par):
                        pool.wait_ge(v_ready, b + 1)
                        pool.wait_ge(o_ps, PRIMED + b)
                        for c in range(NC):
                            pool.tensor_tensor(out=VX[:, :, :, c, :].rearrange("p q h f -> p (q h) f"),
                                               in0=VN[par].rearrange("p q h f -> p (q h) f"),
                                               in1=chm[:, c:c + 1].unsqueeze(2).broadcast_to([P, NQ * HEADS, E + 1]),
                                               op=ALU.mult).then_inc(vx_ready, 1)

                    with pool.Fori(0, B // 2) as i:
                        block_diagonal(2 * i, 0)
                        block_diagonal(2 * i + 1, 1)

        @block.scalar
        def _(act):
            act.wait_ge(const_done, 1)

            def norm(n, token_order):
                def copies(j):
                    for g in (2 * j, 2 * j + 1):
                        act.wait_ge(xT_ps, n * NSH + g + 1)
                        if token_order:
                            dst = XT[:, :].rearrange("d (p i) -> d i p", i=NI)[:, 4 * g:4 * g + 4, :]
                            src = bank[g % 2][:, :].rearrange("d (i p) -> d i p", i=4)
                        else:
                            dst, src = XT[:, 512 * g:512 * g + 512], bank[g % 2][:, :]
                        act.activation(dst, src, ACT.Copy).then_inc(xT_sb, 1)

                for j in range(NG):
                    act.wait_ge(stats_ready, NG * n + j + 1)
                    act.activation(st[:, 3, GI * j:GI * j + GI], mv[:, GI * j:GI * j + GI, 1], ACT.Sqrt,
                                   bias=eps[:, 0:1]).then_inc(std_ready, 1)
                    if j:
                        copies(j - 1)
                copies(NG - 1)

            def ffn(f):
                norm(2 * f, False)
                for g in range(NG):
                    act.wait_ge(shifted, NG * f + g + 1)
                    ex = EX[:, GI * g:GI * g + GI, :]
                    act.activation(ex, ex, ACT.Exp).then_inc(exp_done, 1)

                def shared(g):
                    for k in range(2):
                        n = (f * NSH + g) * 2 + k
                        b1, b3 = shared_banks(g, k)
                        act.wait_ge(sh_ps, n + 1)
                        if n:
                            act.wait_ge(sh_gated, n)
                        act.activation(SH, bank[b1][0:I, :], ACT.Silu).then_inc(sh_copied, 1)
                        act.activation(H3, bank[b3][0:I, :], ACT.Copy).then_inc(sh_copied, 1)
                    act.wait_ge(z_ps, f * NSH + g + 1)
                    if f * NSH + g:
                        act.wait_ge(z_added, f * NSH + g)
                    act.activation(ZB, bank[7][:, :], ACT.Copy, scale=0.5).then_inc(z_read, 1)

                for g in range(NSH):
                    shared(g)

                def copy_xbT(s):
                    act.wait_ge(xbT_ps, f * NS + s + 1)
                    if s >= 2:
                        act.wait_ge(h_ps, f * NS + s - 1)
                    act.activation(XBT[s % 2], bank[(0, 5)[s % 2]][:, 0:P], ACT.Copy).then_inc(xbT_sb, 1)

                def silu(s):
                    act.wait_ge(h_ps, f * NS + s + 1)
                    if s >= 2:
                        act.wait_ge(gated, f * NS + s - 1)
                    act.activation(SG[s % 2], bank[2 + s % 2][:, 0:I], ACT.Silu)\
                        .then_inc(silu_done, 1)

                def copy_gT(s):
                    act.wait_ge(gT_ps, f * NS + s + 1)
                    if s >= 2:
                        act.wait_ge(y_ps, f * NS + s - 1)
                    act.activation(GT[s % 2], bank[(1, 6)[s % 2]][0:I, 0:P], ACT.Copy).then_inc(gT_sb, 1)

                for s in range(NS + 3):
                    if s < NS:
                        copy_xbT(s)
                    if 1 <= s <= NS:
                        silu(s - 1)
                    if 2 <= s <= NS + 1:
                        copy_gT(s - 2)

            ffn(0)

            norm(1, True)
            act.wait_ge(xT_sb, 2 * NSH)
            act.wait_ge(small_in, 16 * N_SMALL)
            act.activation(bq[:, 2:3], bq[:, 2:3], ACT.Copy, scale=QS).then_inc(bq_scaled, 1)
            act.wait_ge(bq_scaled, 1)
            act.sem_inc(kn_sb, PRIMED)

            def slice_h(b):
                act.wait_ge(v_ps, PRIMED + b)
                act.activation(HTB, XT[:, bass.ds(b * L, L)], ACT.Copy).then_inc(hTb_sb, 1)

            def features(b):
                act.wait_ge(qT_ps, b + 1)
                act.wait_ge(q_ready, PRIMED + b)
                act.activation(EQ, bank[0][:, :], ACT.Exp, bias=bq[:, 2:3], scale=QS).then_inc(q_read, 1)
                act.activation(RQ, bank[0][:, :], ACT.Relu, bias=bq[:, 2:3], scale=QS).then_inc(q_read, 1)
                act.wait_ge(kT_ps, b + 1)
                act.wait_ge(k_ready, PRIMED + b)
                act.activation(EK, bank[1][:, :], ACT.Exp, bias=bq[:, 1:2]).then_inc(k_read, 1)
                act.activation(RK, bank[1][:, :], ACT.Relu, bias=bq[:, 1:2]).then_inc(k_read, 1)

            def split_q(b, par):
                act.wait_ge(q_ready, PRIMED + b + 1)
                act.wait_ge(sc_ps, PRIMED + 4 * b)
                for j in range(4):
                    act.activation(Q4[:, j, :], QT[par], ACT.Copy, scale=hm[:, j:j + 1]).then_inc(q4_ready, 1)

            def copy_kn(b):
                act.wait_ge(kn_ps, b + 1)
                act.wait_ge(kv_ps, PRIMED + NQ * b)
                act.activation(KN.rearrange("p q k -> p (q k)"), bank[3][:, :], ACT.Copy).then_inc(kn_sb, 1)

            def copy_anT(b):
                act.wait_ge(anT_ps, PRIMED + b + 1)
                act.wait_ge(pr_ps, PRIMED + b)
                act.activation(AT, bank[3][:, :], ACT.Copy).then_inc(anT_sb, 1)

            def step(b, par, first=False, last=False):
                if not last:
                    features(b + 1)
                    if not (isinstance(b, int) and b + 2 >= B):
                        slice_h(b + 2)
                if not first:
                    copy_anT(b - 1)
                if not last:
                    split_q(b + 1, 1 - par)
                    copy_kn(b + 1)

            slice_h(0)
            features(0)
            slice_h(1)
            split_q(0, 0)
            copy_kn(0)
            step(0, 0, first=True)
            with act.Fori(0, (B - 2) // 2 - 1) as i:
                step(2 * i + 1, 1)
                step(2 * i + 2, 0)
            step(B - 3, 1)
            step(B - 2, 0)
            step(B - 1, 1, last=True)
            copy_anT(B - 1)

            ffn(1)

        @block.tensor
        def _(pe):
            pe.wait_ge(const_done, 1)
            pe.wait_ge(small_in, 16 * N_SMALL)

            def xT(n, g):
                pe.wait_ge(normed, NG * n + g // 2 + 1)
                if g >= 2:
                    pe.wait_ge(xT_sb, n * NSH + g - 1)
                for i in range(4 * g, 4 * g + 4):
                    ins = pe.transpose(bank[g % 2][:, (i % 4) * P:(i % 4 + 1) * P], A[:, i, :], ident[:, :])
                ins.then_inc(xT_ps, 1)

            def ffn(f):
                def logits(g):
                    pe.wait_ge(xT_sb, 2 * f * NSH + 2 * g + 2)
                    for i in range(8 * g, 8 * g + 8):
                        ins = pe.matmul(bank[2 + g][:, (i % 8) * NE:(i % 8 + 1) * NE], XT[:, i * P:(i + 1) * P],
                                        gate_s[:, :], start=True, stop=True)
                    ins.then_inc(logits_ps, 1)

                for g in range(NG):
                    xT(2 * f, 2 * g)
                    xT(2 * f, 2 * g + 1)
                    if g:
                        logits(g - 1)
                logits(NG - 1)

                def shared_hidden(g, k):
                    n = (f * NSH + g) * 2 + k
                    if g == EARLY and k == 0:
                        pe.wait_ge(sh_copied, 2 * n)
                    if g == 0 and k == 1:
                        pe.wait_ge(shifted, NG * (f + 1))
                    if g and g < EARLY:
                        pe.wait_ge(sh_copied, 2 * (n - 1))
                    if g >= EARLY:
                        pe.wait_ge(sh_copied, 2 * n)
                    for w, bk in zip((ws1s, ws3s), shared_banks(g, k)):
                        ins = pe.matmul(bank[bk][0:I, :], w[:, k * I:(k + 1) * I], XT[:, 512 * g:512 * g + 512],
                                        start=True, stop=True)
                    ins.then_inc(sh_ps, 1)

                def shared_out(g):
                    n = f * NSH + g
                    pe.wait_ge(sh_gated, 2 * n + 2)
                    if n:
                        pe.wait_ge(z_read, n)
                    for i in range(4):
                        for k in range(2):
                            ins = pe.matmul(bank[7][:, i * D:(i + 1) * D], HS[k][:, i * P:(i + 1) * P], ws2s[:, k, :],
                                            start=(k == 0), stop=(k == 1))
                    ins.then_inc(z_ps, 1)

                def base():
                    pe.wait_ge(totals, f + 1)
                    pe.matmul(bank[6][:, 0:NE], before[:, :], st2[:, 1, :], start=True, stop=True).then_inc(base_ps, 1)

                def look_up():
                    pe.wait_ge(sh_copied, 4 * (f * NSH + EARLY))
                    for s in range(NS):
                        if s % (NS // 2) == 0:
                            pe.wait_ge(table_ready, 2 * f + s // (NS // 2) + 1)
                        for k in range(2):
                            e = 2 * s + k
                            ins = pe.matmul(bank[2 + s // PER][CAP * k:CAP * k + CAP, (s % PER) * RW:(s % PER + 1) * RW],
                                            OH[:, e, :], R[:, e, :], start=True, stop=True)
                        if s % PER == PER - 1 or s == NS - 1:
                            ins.then_inc(look_ps, 1)

                for g in range(EARLY):
                    for k in range(2):
                        shared_hidden(g, k)
                        if k == 0 and g:
                            shared_out(g - 1)
                    if g == BASE_AFTER:
                        base()
                shared_out(EARLY - 1)
                look_up()
                for g in range(EARLY, NSH):
                    for k in range(2):
                        shared_hidden(g, k)
                    shared_out(g)
                pe.wait_ge(sh_copied, 4 * (f + 1) * NSH)
                pe.wait_ge(z_read, (f + 1) * NSH)
                pe.wait_ge(slots_ready, f + 1)
                pe.wait_ge(w_in, 48 + 16 * f)

                def xb_turn(s):
                    pe.wait_ge(gathered[s % 8], 16 * (f * (NS // 8) + s // 8 + 1))
                    if s >= 2:
                        pe.wait_ge(xbT_sb, f * NS + s - 1)
                    pe.transpose(bank[(0, 5)[s % 2]][:, 0:P], A[:, s, :], ident[:, :]).then_inc(xbT_ps, 1)

                def hidden(s):
                    pe.wait_ge(xbT_sb, f * NS + s + 1)
                    if s >= 2:
                        pe.wait_ge(gated, f * NS + s - 1)
                    for w, off in ((w1s, 0), (w3s, I)):
                        for k in range(2):
                            ins = pe.matmul(bank[2 + s % 2][CAP * k:CAP * k + CAP, off:off + I], XBT[s % 2][:, CAP * k:CAP * k + CAP],
                                            w[:, 2 * s + k, :], start=True, stop=True)
                    ins.then_inc(h_ps, 1)

                def g_turn(s):
                    pe.wait_ge(gated, f * NS + s + 1)
                    if s >= 2:
                        pe.wait_ge(gT_sb, f * NS + s - 1)
                    pe.transpose(bank[(1, 6)[s % 2]][0:I, 0:P], GA[s % 2], ident[:, :]).then_inc(gT_ps, 1)

                def expert_out(s):
                    pe.wait_ge(gT_sb, f * NS + s + 1)
                    if s >= 2:
                        pe.wait_ge(y_sb, f * NS + s - 1)
                    for k in range(2):
                        ins = pe.matmul(bank[(4, 7)[s % 2]][CAP * k:CAP * k + CAP, 0:D], GT[s % 2][:, CAP * k:CAP * k + CAP],
                                        w2s[:, 2 * s + k, :], start=True, stop=True)
                    ins.then_inc(y_ps, 1)

                for s in range(NS + 3):
                    if s < NS:
                        xb_turn(s)
                    if 1 <= s <= NS:
                        hidden(s - 1)
                    if 2 <= s <= NS + 1:
                        g_turn(s - 2)
                    if s >= 3:
                        expert_out(s - 3)

            ffn(0)

            for g in range(NSH):
                xT(1, g)
            pe.wait_ge(xT_sb, 2 * NSH)
            for s in (v_ps, sc_ps, kv_ps, pr_ps, o_ps, anT_ps):
                pe.sem_inc(s, PRIMED)

            def project(b):
                pe.wait_ge(hTb_sb, b + 1)
                if not (isinstance(b, int) and b == 0):
                    pe.wait_ge(kv_sb, PRIMED + 2 * NQ * (b - 1))
                    pe.wait_ge(q_read, 2 * b)
                    pe.wait_ge(v_ready, b)
                    pe.wait_ge(k_read, 2 * b)
                pe.matmul(bank[0][:, :], wqkv[:, 0:D], HTB, start=True, stop=True).then_inc(qT_ps, 1)
                pe.matmul(bank[1][:, :], wqkv[:, D:2 * D], HTB, start=True, stop=True).then_inc(kT_ps, 1)
                for q in range(NQ):
                    ins = pe.matmul(bank[2][:, q * D:(q + 1) * D], HTB[:, q * P:(q + 1) * P], wqkv[:, 2 * D:3 * D],
                                    start=True, stop=True)
                ins.then_inc(v_ps, 1)

            def turn_k(b):
                if not (isinstance(b, int) and b == 0):
                    pe.wait_ge(oo_ready, PRIMED + b - 1)
                pe.wait_ge(k_ready, PRIMED + b + 1)
                for q in range(NQ):
                    ins = pe.transpose(bank[3][:, q * P:(q + 1) * P], KT[:, q * P:(q + 1) * P], ident[:, :])
                ins.then_inc(kn_ps, 1)

            def turn_out(b):
                if not (isinstance(b, int) and b == B - 1):
                    pe.wait_ge(kn_sb, PRIMED + b + 2)
                pe.wait_ge(an_ready, 2 * (b + 1))
                for c in range(NC):
                    ins = pe.transpose(bank[3][:, c * P:(c + 1) * P], AN[:, c, :], ident[:, :])
                ins.then_inc(anT_ps, 1)

            def project_out(b):
                pe.wait_ge(anT_sb, b + 1)
                for c in range(NC):
                    ins = pe.matmul(bank[3][:, c * D:(c + 1) * D], AT[:, c * P:(c + 1) * P], wout[:, :],
                                    start=True, stop=True)
                ins.then_inc(pr_ps, 1)

            def step(b, par, first=False, last=False):
                if not last:
                    project(b + 1)
                pe.wait_ge(q4_ready, 4 * b + 4)
                pe.wait_ge(k_ready, PRIMED + b + 1)
                if not first:
                    turn_out(b - 1)
                for g in range(4):
                    rows = slice(32 * g, 32 * g + 32)
                    for q in range(NQ):
                        for c in range(NC):
                            t0 = q * P + c * CHUNK
                            ins = pe.matmul(bank[4 + g][CHUNK * c:CHUNK * c + CHUNK, q * P:(q + 1) * P]
                                            .rearrange("p (j t) -> p j t", j=4),
                                            KT[rows, t0:t0 + CHUNK], Q4[rows, :, t0:t0 + CHUNK],
                                            start=True, stop=True)
                    ins.then_inc(sc_ps, 1)
                pe.wait_ge(kn_sb, PRIMED + b + 1)
                if last:
                    pe.wait_ge(v_ready, b + 1)
                else:
                    pe.wait_ge(q_read, 2 * (b + 2))
                    pe.wait_ge(v_ready, b + 2)
                for q in range(NQ):
                    if q == 1:
                        pe.wait_ge(sc_sb, 4 * b + 4)
                    if q >= 2:
                        pe.wait_ge(kv_sb, PRIMED + 2 * NQ * b + 2 * (q - 1))
                    for c in range(NC):
                        k = CHUNK * (c + 1)
                        ins = pe.matmul(bank[STATES[q % 2][c // 2]][:, (c % 2) * VW:(c % 2 + 1) * VW], KN[0:k, q, :],
                                        VN[par][0:k, q, :, :].rearrange("p h f -> p (h f)"), start=True, stop=True)
                    ins.then_inc(kv_ps, 1)
                if not first:
                    project_out(b - 1)
                pe.wait_ge(vx_ready, PRIMED + NC * (b + 1))
                pe.wait_ge(sc_sb, 4 * b + 4)
                for h in range(HEADS):
                    ob = bank[4 + h // 8][:, 0:NC * HV].rearrange("p (c h f) -> p c h f", c=NC, h=8)
                    for q in range(NQ):
                        o = (h // 4) * L + q * P + (h % 4) * CHUNK
                        pe.matmul(ob[32 * q:32 * q + 32, :, h % 8, :], PR[:, o:o + CHUNK],
                                  VX[:, q, h, :, :], start=(h % 8 == 0), stop=False, skip_group_check=True)
                pe.wait_ge(kv_sb, PRIMED + 2 * NQ * (b + 1))
                pe.wait_ge(sb_ready, PRIMED + NQ * (b + 1))
                for half in range(2):
                    for c in range(NC):
                        for q in range(NQ):
                            t0 = q * P + c * CHUNK
                            dst = bank[4 + half][32 * q:32 * q + 32, c * HV:(c + 1) * HV]
                            if q:
                                ins = pe.matmul(dst, QT[par][:, t0:t0 + CHUNK], SB[:, q, half * HV:(half + 1) * HV],
                                                start=False, stop=(c == 0), skip_group_check=True)
                            if c:
                                ins = pe.matmul(dst, QT[par][:, t0:t0 + CHUNK], SW[:, q, c - 1, half * HV:(half + 1) * HV],
                                                start=False, stop=True, skip_group_check=True)
                ins.then_inc(o_ps, 1)
                if not last:
                    turn_k(b + 1)

            project(0)
            turn_k(0)
            step(0, 0, first=True)
            with pe.Fori(0, (B - 2) // 2) as i:
                step(2 * i + 1, 1)
                step(2 * i + 2, 0)
            step(B - 1, 1, last=True)
            turn_out(B - 1)
            project_out(B - 1)

            ffn(1)

        @block.vector
        def _(dve):
            steps = [0]

            def then(ins):
                steps[0] += 1
                ins.then_inc(dve_step, 1)
                dve.wait_ge(dve_step, steps[0])

            def over(v, n):
                return v.unsqueeze(2).broadcast_to([P, v.shape[1], n])

            dve.memset(zeros[:, :], 0.0).then_inc(zero_set, 1)
            dve.memset(top8[:, :, :], 0.0)

            def norm(n):
                def update(g):
                    xg = X[:, GI * g:GI * g + GI, :].rearrange("p i d -> p (i d)")
                    cols = slice(g * GI * D, (g + 1) * GI * D)
                    if n == 0:
                        dve.wait_ge(part_in[g], 16)
                        return
                    if n == 2:
                        dve.wait_ge(attn_in, 16 * B)
                        then(dve.tensor_tensor(xg, xg, PL[:, cols], ALU.add))
                        return
                    dve.wait_ge(z_added, NSH * (1 + n // 2))
                    dve.wait_ge(part_in[g], 16 + 64 * (1 + n // 2))
                    for buf in PLANES:
                        then(dve.tensor_tensor(xg, xg, buf[:, cols], ALU.add))
                    dve.memset(st[:, 0, 0:1], 0.0).then_inc(group_ready, 1)

                def stats(g):
                    for i in range(GI * g, GI * g + GI):
                        ins = dve.bn_stats(bn[:, i, :], X[:, i, :])
                    then(ins)
                    for i in range(GI * g, GI * g + GI):
                        ins = dve.bn_aggr(mv[:, i, :], bn[:, i, :])
                    ins.then_inc(stats_ready, 1)

                def normalise(g):
                    dve.wait_ge(std_ready, NG * n + g + 1)
                    cols = slice(GI * g, GI * g + GI)
                    then(dve.reciprocal(st[:, 4, cols], st[:, 3, cols]))
                    for i in range(GI * g, GI * g + GI):
                        ins = dve.tensor_scalar(A[:, i, :], X[:, i, :], mv[:, i, 0:1], st[:, 4, i:i + 1],
                                                ALU.subtract, ALU.mult)
                    ins.then_inc(normed, 1)

                for g in range(NG):
                    update(g)
                    if n < 3:
                        stats(g)
                        if g:
                            normalise(g - 1)
                if n < 3:
                    normalise(NG - 1)

            def ffn(f):
                norm(2 * f)
                if f == 0:
                    dve.wait_ge(const_done, 1)
                    dve.wait_ge(small_in, 16 * N_SMALL)
                for g in range(NG):
                    dve.wait_ge(logits_ps, NG * f + g + 1)
                    lg = bank[2 + g][:, :].rearrange("p (i e) -> p i e", i=GI)
                    tiles = slice(GI * g, GI * g + GI)
                    then(dve.tensor_reduce(st[:, 5, tiles], lg, AX, ALU.max))
                    dve.tensor_tensor(EX[:, tiles, :], lg, over(st[:, 5, tiles], NE), ALU.subtract).then_inc(shifted, 1)
                for g in range(NG):
                    dve.wait_ge(exp_done, NG * f + g + 1)
                    tiles = slice(GI * g, GI * g + GI)
                    ins = dve.tensor_reduce(st[:, 6, tiles], EX[:, tiles, :], AX, ALU.add)
                then(ins)
                then(dve.reciprocal(st[:, 7, :], st[:, 6, :]))
                scores = R[:, :, NI:2 * NI].rearrange("p e i -> p i e")
                then(dve.tensor_tensor(scores, EX, over(st[:, 7, :], NE), ALU.mult))
                dve.tensor_tensor(BI[:, :, 0:NE], scores, gateb[:, :].unsqueeze(1).broadcast_to([P, NI, NE]), ALU.add)
                dve.memset(BI[:, :, NE:NE + 1], -1e30)
                then(dve.memset(BI[:, :, NE + 1:NE + 2], -2e30))
                for i in range(NI):
                    ins = dve.max(top8[:, i, :], BI[:, i, 0:NE])
                then(ins)
                dve.memset(top8[:, :, TOPK:TOPK + 1], -1e30)
                then(dve.memset(top8[:, :, TOPK + 1:TOPK + 2], -2e30))
                for i in range(NI):
                    ins = dve.match_replace(RP[:, i, :], top8[:, i, :], BI[:, i, :], -3e30)
                then(ins)
                then(dve.tensor_tensor(M.rearrange("p e i -> p i e"), RP[:, :, 0:NE], BI[:, :, 0:NE], ALU.not_equal))
                dve.wait_ge(rows_out, 16 * NG * (f + 1))
                dve.wait_ge(xT_ps, (2 * f + 1) * NSH)
                then(dve.tensor_tensor_scan(A_flat[:, 0:NE * NI], Eb[:, :], Eb[:, :], 0.0, ALU.add, ALU.max))
                dve.memset(st2[:, 0, 0:1], 0.0)
                then(dve.tensor_copy(st2[:, 0, 1:NE], CUM[:, 0:NE - 1, NI - 1]))
                dve.tensor_tensor(st2[:, 1, :], CUM[:, :, NI - 1], st2[:, 0, :], ALU.subtract).then_inc(totals, 1)
                dve.wait_ge(base_ps, f + 1)
                then(dve.tensor_copy(st2[:, 2, :], bank[6][:, 0:NE]))
                then(dve.tensor_tensor(st2[:, 3, :], st2[:, 2, :], st2[:, 1, :], ALU.add))
                then(dve.tensor_tensor(st2[:, 4, :], st2[:, 2, :], st2[:, 0, :], ALU.subtract))
                dve.tensor_tensor(R[:, :, 0:NI], CUM, over(st2[:, 4, :], NI), ALU.add)
                then(dve.tensor_scalar(R[:, :, 2 * NI], st2[:, 0, :], 0.0, tok0[:, 0:1], ALU.mult, ALU.add))
                then(dve.tensor_scalar(bnd[:, :, :], st2[:, 2:4, :], float(CAP), None, ALU.min))
                for h in range(2):
                    ex = slice(HE * h, HE * h + HE)
                    c_h = slot_ce[:, :, ex]
                    dve.tensor_tensor(GE, c_h, bnd[:, 0:1, ex].broadcast_to([P, CAP, HE]), ALU.is_ge)
                    then(dve.tensor_tensor(LT, c_h, bnd[:, 1:2, ex].broadcast_to([P, CAP, HE]), ALU.is_lt))
                    ins = dve.tensor_tensor(OH[:, ex, :].rearrange("p e c -> p c e"), GE, LT, ALU.mult)
                    ins.then_inc(table_ready, 1)
                    dve.wait_ge(table_ready, 2 * f + h + 1)
                for s0 in range(0, NS, PER):
                    n = min(PER, NS - s0)
                    dve.wait_ge(look_ps, f * -(-NS // PER) + s0 // PER + 1)
                    bk = bank[2 + s0 // PER][:, 0:n * RW].rearrange("p (s r) -> p s r", s=n)
                    dve.tensor_scalar(LE[:, s0:s0 + n, :], bk[:, :, 0:NI], c_of_p[:, 0:1], None, ALU.is_le)
                    dve.tensor_copy(sl[:, 1, s0:s0 + n], bk[:, :, 2 * NI])
                    ins = dve.tensor_copy(G[:, s0:s0 + n, :], bk[:, :, NI:2 * NI])
                then(ins)
                then(dve.tensor_reduce(sl[:, 0, :], LE, AX, ALU.add))
                then(dve.tensor_tensor(LE, col_i[:, :].unsqueeze(1).broadcast_to([P, NS, NI]), over(sl[:, 0, :], NI),
                                       ALU.is_equal))
                then(dve.tensor_tensor(LE, LE, G, ALU.mult))
                then(dve.tensor_reduce(sl[:, 2, :], LE, AX, ALU.add))
                then(dve.tensor_scalar(sl[:, 2, :], sl[:, 2, :], 0.5, None, ALU.mult))
                then(dve.tensor_tensor(sl[:, 0, :], sl[:, 0, :], sl[:, 1, :], ALU.add))
                then(dve.tensor_scalar(sl[:, 0, :], sl[:, 0, :], -NONE, None, ALU.add))
                then(dve.tensor_copy(tok_i[:, :], sl[:, 0, :]))
                odd = sl[:, 0, :].rearrange("p (s k) -> p s k", k=2)[:, :, 1]
                then(dve.tensor_scalar(odd, odd, 2.0 * T, None, ALU.add))
                then(dve.tensor_scalar(sl[:, 0, :], sl[:, 0, :], plane0[:, 0:1], None, ALU.add))
                then(dve.tensor_copy(put_i[:, :], sl[:, 0, :]))
                dve.memset(st[:, 0, :], 0.0).then_inc(slots_ready, 1)

                def gate(s):
                    dve.wait_ge(silu_done, f * NS + s + 1)
                    if s >= 2:
                        dve.wait_ge(gT_ps, f * NS + s - 1)
                    dve.tensor_tensor(GA[s % 2], SG[s % 2], bank[2 + s % 2][:, I:2 * I], ALU.mult).then_inc(gated, 1)

                def weigh(s):
                    dve.wait_ge(y_ps, f * NS + s + 1)
                    dve.tensor_scalar(Y[:, s, :], bank[(4, 7)[s % 2]][:, 0:D], sl[:, 2, s:s + 1], None, ALU.mult).then_inc(y_sb, 1)

                for s in range(NS + 3):
                    if 1 <= s <= NS:
                        gate(s - 1)
                    if s >= 3:
                        weigh(s - 3)
            ffn(0)

            norm(1)
            for v in VN:
                then(dve.memset(v, 1.0))
            then(dve.memset(SB[:, 0, :], 0.0))
            for s in (q_ready, k_ready, kv_sb, oo_ready, sb_ready):
                dve.sem_inc(s, PRIMED)

            def feature(b, k, e, r, dst, last_readers):
                dve.wait_ge((q_read, k_read)[k], 2 * (b + 1))
                dve.tensor_scalar(e, e, 1.0, FEAT_EPS, ALU.min, ALU.add).then_inc(phi_step, 1)
                dve.wait_ge(phi_step, 2 * b + k + 1)
                dve.wait_ge(*last_readers)
                dve.tensor_tensor(dst, e, r, ALU.add).then_inc((q_ready, k_ready)[k], 1)

            def value(b, par):
                dve.wait_ge(v_ps, PRIMED + b + 1)
                if not (isinstance(b, int) and b < 2):
                    dve.wait_ge(vx_ready, PRIMED + NC * (b - 1))
                    dve.wait_ge(kv_ps, PRIMED + NQ * (b - 1))
                dve.tensor_tensor(VN[par][:, :, :, 0:E],
                                  bank[2][:, :].rearrange("p (q h f) -> p q h f", q=NQ, h=HEADS),
                                  bv[:, :].rearrange("p (h f) -> p h f", h=HEADS).unsqueeze(1)
                                  .broadcast_to([P, NQ, HEADS, E]), ALU.add).then_inc(v_ready, 1)

            def q_feature(b, par):
                n = PRIMED if isinstance(b, int) and b < 2 else PRIMED + b - 1
                feature(b, 0, EQ, RQ, QT[par], (o_ps, n))

            def k_feature(b):
                feature(b, 1, EK, RK, KT, (sc_ps, PRIMED + 4 * b))

            def project_bias(b):
                dve.wait_ge(pr_ps, PRIMED + b + 1)
                dve.wait_ge(oo_stored, PRIMED + b)
                dve.tensor_tensor(OO.rearrange("p (c d) -> p c d", c=NC),
                                  bank[3][:, :].rearrange("p (c d) -> p c d", c=NC),
                                  bo[:, :].unsqueeze(1).broadcast_to([P, NC, D]), ALU.add).then_inc(oo_ready, 1)

            def step(b, par, first=False, last=False):
                if not last:
                    value(b + 1, 1 - par)
                    q_feature(b + 1, 1 - par)
                for g in range(4):
                    dve.wait_ge(sc_ps, PRIMED + 4 * b + g + 1)
                    if g == 0:
                        dve.wait_ge(o_ps, PRIMED + b)
                    dve.tensor_tensor(PR[:, g * L:(g + 1) * L].rearrange("p (n t) -> p n t", t=CHUNK),
                                      bank[4 + g][:, :].rearrange("p (n t) -> p n t", t=CHUNK),
                                      causal[:, :].unsqueeze(1).broadcast_to([P, L // CHUNK, CHUNK]),
                                      ALU.mult).then_inc(sc_sb, 1)
                for q in range(NQ):
                    dve.wait_ge(kv_ps, PRIMED + NQ * b + q + 1)
                    for k in range(2):
                        dve.tensor_tensor(SW[:, q, 2 * k:2 * k + 2, :],
                                          bank[STATES[q % 2][k]][:, 0:2 * VW].rearrange("p (c v) -> p c v", c=2),
                                          own[:, :].unsqueeze(1).broadcast_to([P, 2, VW]), ALU.mult).then_inc(kv_sb, 1)
                    dve.wait_ge(kv_sb, PRIMED + 2 * NQ * b + 2 * q + 2)
                    dve.wait_ge(sb_ready, PRIMED + NQ * b + q)
                    if q < NQ - 1:
                        dve.tensor_tensor(SB[:, q + 1, :], SB[:, q, :], SW[:, q, NC - 1, :], ALU.add).then_inc(sb_ready, 1)
                    else:
                        dve.memset(st[:, 0, 0:1], 0.0).then_inc(sb_ready, 1)
                if not last:
                    k_feature(b + 1)
                if not first:
                    project_bias(b - 1)
                dve.wait_ge(o_ps, PRIMED + b + 1)
                if not first:
                    dve.wait_ge(anT_ps, PRIMED + b)
                for k in range(2):
                    ob = bank[4 + k][:, 0:NC * HV].rearrange("p (n f) -> p n f", f=E + 1)
                    den = top8[:, 8 * k:8 * k + 4, :].rearrange("p a b -> p (a b)")
                    rec = top8[:, 8 * k + 4:8 * k + 8, :].rearrange("p a b -> p (a b)")
                    dve.tensor_scalar(den, ob[:, :, E], DEN_EPS, None, ALU.add).then_inc(o_step, 1)
                    dve.wait_ge(o_step, 4 * b + 2 * k + 1)
                    dve.reciprocal(rec, den).then_inc(o_step, 1)
                    dve.wait_ge(o_step, 4 * b + 2 * k + 2)
                    dve.tensor_tensor(AN[:, :, k * 8 * E:(k + 1) * 8 * E].rearrange("p c (h f) -> p c h f", h=8),
                                      bank[4 + k][:, 0:NC * HV].rearrange("p (c h f) -> p c h f", c=NC, h=8)[:, :, :, 0:E],
                                      rec.rearrange("p (c h) -> p c h", c=NC).unsqueeze(3)
                                      .broadcast_to([P, NC, 8, E]), ALU.mult).then_inc(an_ready, 1)

            value(0, 0)
            q_feature(0, 0)
            k_feature(0)
            step(0, 0, first=True)
            with dve.Fori(0, (B - 2) // 2) as i:
                step(2 * i + 1, 1)
                step(2 * i + 2, 0)
            step(B - 1, 1, last=True)
            project_bias(B - 1)

            ffn(1)
            norm(3)


def kernel(**inputs):
    import numpy as _np
    import concourse.bacc as _bacc
    from concourse import mybir as _mybir
    from concourse.bass_utils import run_bass_kernel_spmd as _run

    a = {k: _np.asarray(v) for k, v in inputs.items()}
    inner = a["L0_ffn_w1"].shape[1]
    laid = {
        "x": a["L0_attn_x"],
        "w_qkv": a["L0_attn_W_qkv"],
        "b_qkv": a["L0_attn_b_qkv"],
        "w_out": a["L0_attn_W_out"],
        "b_out": a["L0_attn_b_out"],
        "gate_wT": a["L0_ffn_gate_w"].T,
        "gate_b": a["L0_ffn_gate_b"],
        "w1T": a["L0_ffn_w1"].transpose(2, 0, 1),
        "w2T": a["L0_ffn_w2"].transpose(2, 0, 1),
        "w3T": a["L0_ffn_w3"].transpose(2, 0, 1),
        "ws1T": a["L0_ffn_ws1"].T,
        "ws2T": a["L0_ffn_ws2"].T.reshape(2, inner, -1).transpose(1, 0, 2),
        "ws3T": a["L0_ffn_ws3"].T,
    }
    nc = _bacc.Bacc("TRN2", target_bir_lowering=False, num_devices=1)
    arrays, args = {}, []
    for name, v in laid.items():
        v = _np.ascontiguousarray(v)
        arrays[f"in_{name}"] = v
        args.append(nc.dram_tensor(f"in_{name}", v.shape, _mybir.dt.from_np(v.dtype), kind="ExternalInput").ap())
    out = nc.dram_tensor("out_x", laid["x"].shape, _mybir.dt.from_np(laid["x"].dtype), kind="ExternalOutput").ap()
    macaron_kernel(nc, *args, out)
    r = _run(nc, [arrays], core_ids=[0])
    return r.results[0]["out_x"]
```

```python
from contextlib import ExitStack

import concourse.bass as bass
from concourse import mybir

ALU = mybir.AluOpType
ACT = mybir.ActivationFunctionType
AX = mybir.AxisListType.X
F32 = mybir.dt.float32
BF16 = mybir.dt.bfloat16
I32 = mybir.dt.int32

P = 128
TOPK = 6
CAP = 64
LN_EPS = 1e-5
FEAT_EPS = 1e-4
DEN_EPS = 1e-6
HEADS = 16
CHUNK = 32
NONE = -32768.0


def macaron_kernel(nc, x, w_qkv, b_qkv, w_out, b_out, gate_wT, gate_b, w1T, w2T, w3T, ws1T, ws2T, ws3T, out):
    B, L, D = x.shape
    T = B * L
    NI = T // P
    NE = gate_wT.shape[1]
    I = w1T.shape[2]
    NS = NE * CAP // P
    E = D // HEADS
    VW = HEADS * (E + 1)
    HV = VW // 2
    NQ = L // P
    NC = P // CHUNK
    RW = 2 * NI + 1
    PER = 7
    NB = -(-NS // PER)
    NQT = 4
    NG = 4
    GI = NI // NG
    NSH = NI // 4
    EARLY = NSH
    BASE_AFTER = 3
    COUNTS_AFTER = 5
    QS = float(E) ** -0.5
    STATES = ((0, 2), (6, 7))

    ctx = ExitStack()
    with ctx:
        def sb(name, shape, dt=F32):
            return ctx.enter_context(nc.sbuf_tensor(name, shape, dt))

        def sem(name):
            return ctx.enter_context(nc.semaphore(name))

        rows_d = nc.dram_tensor("rows_d", (T, D), F32, kind="Internal").ap()
        planes_d = [nc.dram_tensor(f"planes{f}_d", (4 * T, D), F32, kind="Internal").ap() for f in range(2)]
        attn_d = nc.dram_tensor("attn_d", (T, D), F32, kind="Internal").ap()

        X = sb("X", [P, NI, D])
        A = sb("A", [P, NI, D])
        XT = sb("XT", [P, T])
        Bb = sb("Bb", [P, NE * RW])
        Cb = sb("Cb", [P, 2 * NI * (NE + 2)])
        Eb = sb("Eb", [P, NE * NI])
        w1s = sb("w1s", [P, NE, I])
        w3s = sb("w3s", [P, NE, I])
        w2s = sb("w2s", [I, NE, D])
        ring = sb("ring", [P, 2 * (P + I + I + P)])
        ident = sb("ident", [P, P])
        before = sb("before", [P, P])
        causal = sb("causal", [P, CHUNK])
        own = sb("own", [P, VW])
        chm = sb("chm", [P, NC])
        hm = sb("hm", [P, 4])
        col_i = sb("col_i", [P, NI])
        c_of_p = sb("c_of_p", [P, 1])
        tok0 = sb("tok0", [P, 1])
        plane0 = sb("plane0", [P, NS])
        twice = sb("twice", [P, P])
        gate_s = sb("gate_s", [P, NE])
        gateb = sb("gateb", [P, NE])
        ws1s = sb("ws1s", [P, 2 * I])
        ws3s = sb("ws3s", [P, 2 * I])
        ws2s = sb("ws2s", [I, 2, D])
        wqkv = sb("wqkv", [P, 3 * D])
        wout = sb("wout", [P, D])
        bq = sb("bq", [P, 3])
        bv = sb("bv", [P, D])
        bo = sb("bo", [P, D])
        st = sb("st", [P, 8, NI])
        top8 = sb("top8", [P, NI, 8])
        st2 = sb("st2", [P, 5, NE])
        sl = sb("sl", [P, 3, NS])
        tok_i = sb("tok_i", [P, NS], I32)
        put_i = sb("put_i", [P, NS], I32)
        eps = sb("eps", [P, 1])
        zeros = sb("zeros", [P, 4 * D])
        PL = sb("PL", [P, NI * D])
        slot_ce = sb("slot_ce", [P, CAP, NE], BF16)
        bnd = sb("bnd", [P, 2, NE], BF16)
        bn = sb("bn", [P, NI, 6])
        mv = sb("mv", [P, NI, 2])

        A_flat = A[:, :, :].rearrange("p i d -> p (i d)")
        R = Bb[:, :].rearrange("p (e r) -> p e r", e=NE)
        Y = Bb[:, 0:NS * D].rearrange("p (s d) -> p s d", s=NS)
        BI = Cb[:, 0:NI * (NE + 2)].rearrange("p (i e) -> p i e", i=NI)
        RP = Cb[:, NI * (NE + 2):2 * NI * (NE + 2)].rearrange("p (i e) -> p i e", i=NI)
        OH = Cb[:, 0:NE * CAP].rearrange("p (e c) -> p e c", e=NE)
        HE = NE // NQT
        GL = [[A_flat[:, 2048 + 512 * (2 * j + k):2560 + 512 * (2 * j + k)].bitcast(BF16)
               .rearrange("p (c e) -> p c e", c=CAP) for k in range(2)] for j in range(2)]
        EX = Eb[:, :].rearrange("p (i e) -> p i e", i=NI)
        M = Eb[:, :].rearrange("p (e i) -> p e i", e=NE)
        CUM = A_flat[:, 0:NE * NI].rearrange("p (e i) -> p e i", e=NE)
        LE = Eb[:, 0:NS * NI].rearrange("p (s i) -> p s i", s=NS)
        XBT = [ring[:, k * P:(k + 1) * P] for k in range(2)]
        o = 2 * P
        SG = [ring[:, o + k * I:o + (k + 1) * I] for k in range(2)]
        o += 2 * I
        GA = [ring[:, o + k * I:o + (k + 1) * I] for k in range(2)]
        o += 2 * I
        GT = [ring[0:I, o + k * P:o + (k + 1) * P] for k in range(2)]

        parts = [PL[0:I, 512 * k:512 * k + 512] for k in range(8)]
        SH, H3, HS = parts[0:2], parts[2:4], (parts[4:6], parts[6:8])

        PR = A_flat[:, 0:4 * L]
        Q4 = A_flat[:, 4 * L:8 * L].rearrange("p (j t) -> p j t", j=4)
        VX = Bb[:, 0:NQ * NC * VW].rearrange("p (q h c f) -> p q h c f", q=NQ, h=HEADS, c=NC)
        o = NQ * NC * VW
        HTB, KT, QT0 = (Bb[:, o + k * L:o + (k + 1) * L] for k in range(3))
        SW = Cb[:, 0:NQ * NC * VW].rearrange("p (q c v) -> p q c v", q=NQ, c=NC)
        SB = Cb[:, o:o + NQ * VW].rearrange("p (q v) -> p q v", q=NQ)
        o += NQ * VW
        VN0 = Cb[:, o:o + NQ * VW]
        o += NQ * VW
        KN = Cb[:, o:o + L].rearrange("p (q k) -> p q k", q=NQ)
        EQ, RQ, AT, OO = (Eb[:, k * L:(k + 1) * L] for k in range(4))
        spare = w3s[:, :, :].rearrange("p e i -> p (e i)")
        QT1, EK, RK = (spare[:, k * L:(k + 1) * L] for k in range(3))
        QT = (QT0, QT1)
        VN = [v.rearrange("p (q h f) -> p q h f", q=NQ, h=HEADS) for v in (VN0, spare[:, 3 * L:3 * L + NQ * VW])]
        AN = ring[:, 0:L].rearrange("p (c k) -> p c k", c=NC)

        bank = [ctx.enter_context(nc.psum_tensor(f"bank{k}", [P, 512], F32)) for k in range(8)]

        part_in = [sem(f"part_in{g}") for g in range(NG)]
        small_in = sem("small_in")
        stats_ready = sem("stats_ready")
        scale_ready = sem("scale_ready")
        recip_ready = sem("recip_ready")
        scores_ready = sem("scores_ready")
        base_ready = sem("base_ready")
        counts_ready = sem("counts_ready")
        sh_copied = sem("sh_copied")
        group_ready = sem("group_ready")
        w_in = sem("w_in")
        zero_set = sem("zero_set")
        planes_zero = sem("planes_zero")
        const_step = sem("const_step")
        const_done = sem("const_done")
        dve_step = sem("dve_step")
        std_ready = sem("std_ready")
        normed = sem("normed")
        xT_ps = sem("xT_ps")
        xT_sb = sem("xT_sb")
        rows_out = sem("rows_out")
        logits_ps = sem("logits_ps")
        shifted = sem("shifted")
        exp_done = sem("exp_done")
        totals = sem("totals")
        base_ps = sem("base_ps")
        table_ready = sem("table_ready")
        look_ps = sem("look_ps")
        slots_ready = sem("slots_ready")
        gathered = [sem(f"gathered{k}") for k in range(8)]
        xbT_ps = sem("xbT_ps")
        xbT_sb = sem("xbT_sb")
        h_ps = sem("h_ps")
        silu_done = sem("silu_done")
        gated = sem("gated")
        gT_ps = sem("gT_ps")
        gT_sb = sem("gT_sb")
        y_ps = sem("y_ps")
        y_sb = sem("y_sb")
        added = [sem(f"added{k}") for k in range(2)]
        sh_ps = sem("sh_ps")
        sh_gated = sem("sh_gated")
        z_ps = sem("z_ps")
        z_added = sem("z_added")
        out_done = sem("out_done")
        PRIMED = 1
        hTb_sb = sem("hTb_sb")
        qT_ps = sem("qT_ps")
        kT_ps = sem("kT_ps")
        v_ps = sem("v_ps")
        bq_scaled = sem("bq_scaled")
        q_read = sem("q_read")
        k_read = sem("k_read")
        phi_step = sem("phi_step")
        q_ready = sem("q_ready")
        k_ready = sem("k_ready")
        q4_ready = sem("q4_ready")
        v_ready = sem("v_ready")
        vx_ready = sem("vx_ready")
        kn_ps = sem("kn_ps")
        kn_sb = sem("kn_sb")
        sc_ps = sem("sc_ps")
        sc_sb = sem("sc_sb")
        kv_ps = sem("kv_ps")
        kv_sb = sem("kv_sb")
        sb_ready = sem("sb_ready")
        o_ps = sem("o_ps")
        o_step = sem("o_step")
        an_ready = sem("an_ready")
        anT_ps = sem("anT_ps")
        anT_sb = sem("anT_sb")
        pr_ps = sem("pr_ps")
        oo_ready = sem("oo_ready")
        attn_out = sem("attn_out")
        oo_stored = sem("oo_stored")
        attn_in = sem("attn_in")

        x_blk = x.rearrange("b l d -> (b l) d").rearrange("(p i) d -> p i d", p=P)
        out_blk = out.rearrange("b l d -> (b l) d").rearrange("(p i) d -> p i d", p=P)
        rows_blk = rows_d.rearrange("(p i) d -> p i d", p=P)
        PLANES = (A_flat, PL[:, :], Cb[:, 0:T], Bb[:, 0:T])
        N_SMALL = 12

        SHARED = ((0, 1), (4, 5))
        block = ctx.enter_context(nc.Block())

        @block.sync
        def _(sp):
            for g in range(NG):
                sp.dma_start(X[:, GI * g:GI * g + GI, :], x_blk[:, GI * g:GI * g + GI, :]).then_inc(part_in[g], 16)
            sp.dma_start(gate_s[:, :], gate_wT).then_inc(small_in, 16)
            sp.dma_start(gateb[:, :], gate_b.rearrange("(a e) -> a e", a=1).broadcast_to([P, NE])).then_inc(small_in, 16)
            sp.dma_start(ws1s[:, :], ws1T).then_inc(small_in, 16)
            sp.dma_start(ws3s[:, :], ws3T).then_inc(small_in, 16)
            sp.dma_start(ws2s[:, :, :], ws2T).then_inc(small_in, 16)
            sp.dma_start(wqkv[:, :], w_qkv).then_inc(small_in, 16)
            sp.dma_start(wout[:, :], w_out).then_inc(small_in, 16)
            sp.dma_start(bq[:, 0:1], b_qkv[0:D].rearrange("(p a) -> p a", a=1)).then_inc(small_in, 16)
            sp.dma_start(bq[:, 1:2], b_qkv[D:2 * D].rearrange("(p a) -> p a", a=1)).then_inc(small_in, 16)
            sp.dma_start(bq[:, 2:3], b_qkv[0:D].rearrange("(p a) -> p a", a=1)).then_inc(small_in, 16)
            sp.dma_start(bv[:, :], b_qkv[2 * D:3 * D].rearrange("(a e) -> a e", a=1).broadcast_to([P, D])).then_inc(small_in, 16)
            sp.dma_start(bo[:, :], b_out.rearrange("(a e) -> a e", a=1).broadcast_to([P, D])).then_inc(small_in, 16)
            def clear_planes(f):
                for k in range(4):
                    dst = planes_d[f][k * T:(k + 1) * T, :].rearrange("(p a i) d -> p a (i d)", p=P, i=4)
                    sp.dma_start(dst, zeros[:, :].unsqueeze(1).broadcast_to([P, NI // 4, 4 * D])).then_inc(planes_zero, 16)

            sp.wait_ge(zero_set, 1)
            clear_planes(0)

            for f in range(2):
                for g in range(NG):
                    sp.wait_ge(normed, NG * 2 * f + g + 1)
                    sp.dma_start(rows_blk[:, GI * g:GI * g + GI, :], A[:, GI * g:GI * g + GI, :]).then_inc(rows_out, 16)
                if f == 0:
                    for dst, src in ((w1s, w1T), (w3s, w3T), (w2s, w2T)):
                        sp.dma_start(dst[:, :, :], src).then_inc(w_in, 16)
                for k in range(2):
                    sp.wait_ge(added[k], 16 * (NS // 2) * (f + 1))
                sp.wait_ge(z_added, NSH * (f + 1))
                for g in range(NG):
                    cols = slice(g * GI * D, (g + 1) * GI * D)
                    for k, buf in enumerate(PLANES):
                        src = planes_d[f][k * T:(k + 1) * T, :].rearrange("(p i) d -> p (i d)", p=P)
                        sp.dma_start(buf[:, cols], src[:, cols]).then_inc(part_in[g], 16)
                if f == 0:
                    clear_planes(1)
                    sp.sem_inc(oo_stored, PRIMED)
                    for b in range(B):
                        sp.wait_ge(oo_ready, PRIMED + b + 1)
                        for q in range(NQ):
                            sp.dma_start(attn_d[b * L + q * P:b * L + (q + 1) * P, :].rearrange("(c t) d -> t c d", t=CHUNK),
                                         OO[32 * q:32 * q + 32, :].rearrange("p (c d) -> p c d", c=NC)).then_inc(attn_out, 16)
                        sp.wait_ge(attn_out, 16 * NQ * (b + 1))
                        sp.sem_inc(oo_stored, 1)
                        rows = slice(P // B * b, P // B * (b + 1))
                        sp.wait_ge(group_ready, NG)
                        sp.dma_start(PL[rows, :], attn_d[b * L:(b + 1) * L, :].rearrange("(p i) d -> p (i d)", p=P // B))\
                            .then_inc(attn_in, 16)
                    sp.dma_start(w3s[:, :, :], w3T).then_inc(w_in, 16)
            for g in range(NG):
                sp.wait_ge(group_ready, NG + g + 1)
                sp.dma_start(out_blk[:, GI * g:GI * g + GI, :], X[:, GI * g:GI * g + GI, :]).then_inc(out_done, 16)
            sp.wait_ge(out_done, 16 * NG)
            sp.wait_ge(planes_zero, 16 * 8)

        @block.gpsimd
        def _(pool):
            made = [0]

            def then(ins):
                made[0] += 1
                ins.then_inc(const_step, 1)
                pool.wait_ge(const_step, made[0])

            def keep(t, op, base, pattern, per_partition, fill):
                then(pool.affine_select(out=t, in_=t, compare_op=op, fill=fill, base=base, pattern=pattern,
                                        channel_multiplier=per_partition))

            def count(t, base, pattern, per_partition):
                then(pool.iota(t, pattern=pattern, base=base, channel_multiplier=per_partition,
                               allow_small_or_imprecise_dtypes=True))

            then(pool.memset(eps[:, :], LN_EPS))
            then(pool.memset(ident[:, :], 0.0))
            keep(ident[:, :], ALU.not_equal, 0, [[-1, P]], 1, 1.0)
            then(pool.memset(twice[:, :], 0.0))
            keep(twice[:, :], ALU.not_equal, 0, [[-1, P]], 1, 2.0)
            then(pool.memset(before[:, :], 1.0))
            keep(before[:, :], ALU.is_gt, 0, [[1, P]], -1, 0.0)
            then(pool.memset(causal[:, :], 1.0))
            for c in range(NC):
                keep(causal[CHUNK * c:CHUNK * c + CHUNK, :], ALU.is_ge, 0, [[1, CHUNK]], -1, 0.0)
            then(pool.memset(own[:, :], 1.0))
            ov = own[:, :].rearrange("p (h f) -> p h f", h=HEADS)
            keep(ov, ALU.is_ge, 0, [[-E, HEADS], [0, E + 1]], 1, 0.0)
            keep(ov, ALU.is_ge, E - 1, [[E, HEADS], [0, E + 1]], -1, 0.0)
            then(pool.memset(chm[:, :], 1.0))
            keep(chm[:, :], ALU.is_ge, 0, [[-CHUNK, NC]], 1, 0.0)
            keep(chm[:, :], ALU.is_ge, CHUNK - 1, [[CHUNK, NC]], -1, 0.0)
            own3 = own[:, :].rearrange("p (g j f) -> p j g f", g=4, j=4)
            then(pool.tensor_tensor(out=hm[:, :], in0=own3[:, :, 0, 0], in1=own3[:, :, 1, 0], op=ALU.add))
            for k in (2, 3):
                then(pool.tensor_tensor(out=hm[:, :], in0=hm[:, :], in1=own3[:, :, k, 0], op=ALU.add))
            count(col_i[:, :], 0, [[1, NI]], 0)
            for k in range(2):
                count(c_of_p[k * CAP:(k + 1) * CAP, :], 0, [[0, 1]], 1)
                count(plane0[k * CAP:(k + 1) * CAP, :], k * T, [[0, NS // 2], [2 * T, 2]], 0)
            count(tok0[:, :], int(NONE), [[0, 1]], NI)
            count(slot_ce[:, :, :], 0, [[1, CAP], [0, NE]], 0)
            pool.memset(st2[:, 0, :], 0.0).then_inc(const_done, 1)

            for f in range(2):
                for g in range(NG):
                    pool.wait_ge(recip_ready, NG * f + g + 1)
                    tiles = slice(GI * g, GI * g + GI)
                    pool.tensor_tensor(out=R[:, :, NI:2 * NI].rearrange("p e i -> p i e")[:, tiles, :], in0=EX[:, tiles, :],
                                       in1=st[:, 7, tiles].unsqueeze(2).broadcast_to([P, GI, NE]),
                                       op=ALU.mult).then_inc(scores_ready, 1)

                def counts():
                    for h in range(NQT):
                        ex = slice(HE * h, HE * h + HE)
                        pool.wait_ge(base_ready, f + 1)
                        pool.tensor_tensor(out=R[:, ex, 0:NI], in0=CUM[:, ex, :],
                                           in1=st2[:, 4, ex].unsqueeze(2).broadcast_to([P, HE, NI]),
                                           op=ALU.add).then_inc(counts_ready, 1)

                for g in range(NSH):
                    for k in range(2):
                        n = (f * NSH + g) * 2 + k
                        pool.wait_ge(sh_copied, 2 * n + 2)
                        if g >= 2:
                            pool.wait_ge(z_ps, f * NSH + g - 1)
                        pool.tensor_tensor(out=HS[g % 2][k], in0=SH[k], in1=H3[k], op=ALU.mult).then_inc(sh_gated, 1)
                    if g == COUNTS_AFTER:
                        counts()
                pool.wait_ge(counts_ready, NQT * (f + 1))
                pool.wait_ge(rows_out, 16 * NG * (f + 1))
                pool.wait_ge(planes_zero, 16 * 4 * (f + 1))

                def add(s):
                    pool.wait_ge(y_sb, f * NS + s + 1)
                    n = f * (NS // 2) + s // 2
                    if n:
                        pool.wait_ge(added[s % 2], 16 * n)
                    pool.indirect_dma_start(out=planes_d[f], in_=Y[:, s, :], in_offset=None,
                                            out_offset=bass.IndirectOffsetOnAxis(ap=put_i[:, s:s + 1], axis=0),
                                            bounds_check=4 * T - 1, oob_is_err=False,
                                            compute_op=ALU.add).then_inc(added[s % 2], 16)

                LAG = 6
                for s in range(NS + LAG):
                    if s < NS:
                        pool.wait_ge(slots_ready, NB * f + s // PER + 1)
                        n = f * (NS // 8) + s // 8
                        if n:
                            pool.wait_ge(gathered[s % 8], 16 * n)
                        pool.indirect_dma_start(out=A[:, s, :], out_offset=None, in_=rows_d,
                                                in_offset=bass.IndirectOffsetOnAxis(ap=tok_i[:, s:s + 1], axis=0),
                                                bounds_check=T - 1, oob_is_err=False).then_inc(gathered[s % 8], 16)
                    if s >= LAG:
                        add(s - LAG)
                if f == 0:
                    pool.wait_ge(group_ready, NG)
                    pool.sem_inc(vx_ready, PRIMED)

                    def block_diagonal(b, par):
                        pool.wait_ge(v_ready, b + 1)
                        pool.wait_ge(o_ps, PRIMED + b)
                        for c in range(NC):
                            pool.tensor_tensor(out=VX[:, :, :, c, :].rearrange("p q h f -> p (q h) f"),
                                               in0=VN[par].rearrange("p q h f -> p (q h) f"),
                                               in1=chm[:, c:c + 1].unsqueeze(2).broadcast_to([P, NQ * HEADS, E + 1]),
                                               op=ALU.mult).then_inc(vx_ready, 1)

                    with pool.Fori(0, B // 2) as i:
                        block_diagonal(2 * i, 0)
                        block_diagonal(2 * i + 1, 1)

        @block.scalar
        def _(act):
            act.wait_ge(const_done, 1)

            def norm(n, token_order):
                def copies(j):
                    for g in (2 * j, 2 * j + 1):
                        act.wait_ge(xT_ps, n * NSH + g + 1)
                        if token_order:
                            dst = XT[:, :].rearrange("d (p i) -> d i p", i=NI)[:, 4 * g:4 * g + 4, :]
                            src = bank[g % 2][:, :].rearrange("d (i p) -> d i p", i=4)
                        else:
                            dst, src = XT[:, 512 * g:512 * g + 512], bank[g % 2][:, :]
                        act.activation(dst, src, ACT.Copy).then_inc(xT_sb, 1)

                def normalise(j):
                    act.wait_ge(scale_ready, NG * n + j + 1)
                    for i in range(GI * j, GI * j + GI):
                        ins = act.activation(A[:, i, :], X[:, i, :], ACT.Identity, bias=st[:, 1, i:i + 1],
                                             scale=st[:, 4, i:i + 1])
                    ins.then_inc(normed, 1)

                for j in range(NG + 1):
                    if j < NG:
                        act.wait_ge(stats_ready, NG * n + j + 1)
                        act.activation(st[:, 3, GI * j:GI * j + GI], mv[:, GI * j:GI * j + GI, 1], ACT.Sqrt,
                                       bias=eps[:, 0:1]).then_inc(std_ready, 1)
                    if j:
                        normalise(j - 1)
                    if j >= 2:
                        copies(j - 2)
                copies(NG - 1)

            def ffn(f):
                norm(2 * f, False)
                for g in range(NG):
                    act.wait_ge(shifted, NG * f + g + 1)
                    ex = EX[:, GI * g:GI * g + GI, :]
                    act.activation(ex, ex, ACT.Exp).then_inc(exp_done, 1)

                def shared_copies(g):
                    for k in range(2):
                        n = (f * NSH + g) * 2 + k
                        b1, b3 = SHARED[k]
                        act.wait_ge(sh_ps, n + 1)
                        if n >= 2:
                            act.wait_ge(sh_gated, n - 1)
                        act.activation(SH[k], bank[b1][0:I, :], ACT.Silu).then_inc(sh_copied, 1)
                        act.activation(H3[k], bank[b3][0:I, :], ACT.Copy).then_inc(sh_copied, 1)

                def shared_add(g):
                    act.wait_ge(z_ps, f * NSH + g + 1)
                    act.activation(X[:, 4 * g:4 * g + 4, :].rearrange("p i d -> p (i d)"), bank[7][:, :], ACT.Copy,
                                   scale=0.5).then_inc(z_added, 1)

                for g in range(NSH + 1):
                    if g < NSH:
                        shared_copies(g)
                    if g:
                        shared_add(g - 1)

                def copy_xbT(s):
                    act.wait_ge(xbT_ps, f * NS + s + 1)
                    if s >= 2:
                        act.wait_ge(h_ps, f * NS + s - 1)
                    act.activation(XBT[s % 2], bank[(0, 5)[s % 2]][:, 0:P], ACT.Copy).then_inc(xbT_sb, 1)

                def silu(s):
                    act.wait_ge(h_ps, f * NS + s + 1)
                    if s >= 2:
                        act.wait_ge(gated, f * NS + s - 1)
                    act.activation(SG[s % 2], bank[2 + s % 2][:, 0:I], ACT.Silu)\
                        .then_inc(silu_done, 1)

                def copy_gT(s):
                    act.wait_ge(gT_ps, f * NS + s + 1)
                    if s >= 2:
                        act.wait_ge(y_ps, f * NS + s - 1)
                    act.activation(GT[s % 2], bank[(1, 6)[s % 2]][0:I, 0:P], ACT.Copy).then_inc(gT_sb, 1)

                for s in range(NS + 3):
                    if s < NS:
                        copy_xbT(s)
                    if 1 <= s <= NS:
                        silu(s - 1)
                    if 2 <= s <= NS + 1:
                        copy_gT(s - 2)

            ffn(0)

            norm(1, True)
            act.wait_ge(xT_sb, 2 * NSH)
            act.wait_ge(small_in, 16 * N_SMALL)
            act.activation(bq[:, 2:3], bq[:, 2:3], ACT.Copy, scale=QS).then_inc(bq_scaled, 1)
            act.wait_ge(bq_scaled, 1)
            act.sem_inc(kn_sb, PRIMED)

            def slice_h(b):
                act.wait_ge(v_ps, PRIMED + b)
                act.activation(HTB, XT[:, bass.ds(b * L, L)], ACT.Copy).then_inc(hTb_sb, 1)

            def features(b):
                act.wait_ge(qT_ps, b + 1)
                act.wait_ge(q_ready, PRIMED + b)
                act.activation(EQ, bank[0][:, :], ACT.Exp, bias=bq[:, 2:3], scale=QS).then_inc(q_read, 1)
                act.activation(RQ, bank[0][:, :], ACT.Relu, bias=bq[:, 2:3], scale=QS).then_inc(q_read, 1)
                act.wait_ge(kT_ps, b + 1)
                act.wait_ge(k_ready, PRIMED + b)
                act.activation(EK, bank[1][:, :], ACT.Exp, bias=bq[:, 1:2]).then_inc(k_read, 1)
                act.activation(RK, bank[1][:, :], ACT.Relu, bias=bq[:, 1:2]).then_inc(k_read, 1)

            def split_q(b, par):
                act.wait_ge(q_ready, PRIMED + b + 1)
                act.wait_ge(sc_ps, PRIMED + 4 * b)
                for j in range(4):
                    act.activation(Q4[:, j, :], QT[par], ACT.Copy, scale=hm[:, j:j + 1]).then_inc(q4_ready, 1)

            def copy_kn(b):
                act.wait_ge(kn_ps, b + 1)
                act.wait_ge(kv_ps, PRIMED + NQ * b)
                act.activation(KN.rearrange("p q k -> p (q k)"), bank[3][:, :], ACT.Copy).then_inc(kn_sb, 1)

            def copy_anT(b):
                act.wait_ge(anT_ps, PRIMED + b + 1)
                act.wait_ge(pr_ps, PRIMED + b)
                act.activation(AT, bank[3][:, :], ACT.Copy).then_inc(anT_sb, 1)

            def step(b, par, first=False, last=False):
                if not last:
                    features(b + 1)
                    if not (isinstance(b, int) and b + 2 >= B):
                        slice_h(b + 2)
                if not first:
                    copy_anT(b - 1)
                if not last:
                    split_q(b + 1, 1 - par)
                    copy_kn(b + 1)

            slice_h(0)
            features(0)
            slice_h(1)
            split_q(0, 0)
            copy_kn(0)
            step(0, 0, first=True)
            with act.Fori(0, (B - 2) // 2 - 1) as i:
                step(2 * i + 1, 1)
                step(2 * i + 2, 0)
            step(B - 3, 1)
            step(B - 2, 0)
            step(B - 1, 1, last=True)
            copy_anT(B - 1)

            ffn(1)

        @block.tensor
        def _(pe):
            pe.wait_ge(const_done, 1)
            pe.wait_ge(small_in, 16 * N_SMALL)

            def xT(n, g):
                pe.wait_ge(normed, NG * n + g // 2 + 1)
                if g >= 2:
                    pe.wait_ge(xT_sb, n * NSH + g - 1)
                for i in range(4 * g, 4 * g + 4):
                    ins = pe.transpose(bank[g % 2][:, (i % 4) * P:(i % 4 + 1) * P], A[:, i, :], ident[:, :])
                ins.then_inc(xT_ps, 1)

            def ffn(f):
                def logits(g):
                    pe.wait_ge(xT_sb, 2 * f * NSH + 2 * g + 2)
                    for i in range(8 * g, 8 * g + 8):
                        ins = pe.matmul(bank[2 + g][:, (i % 8) * NE:(i % 8 + 1) * NE], XT[:, i * P:(i + 1) * P],
                                        gate_s[:, :], start=True, stop=True)
                    ins.then_inc(logits_ps, 1)

                for g in range(NG):
                    xT(2 * f, 2 * g)
                    xT(2 * f, 2 * g + 1)
                    if g:
                        logits(g - 1)
                logits(NG - 1)

                def shared_hidden(g, k):
                    n = (f * NSH + g) * 2 + k
                    if g == 0 and k == 1:
                        pe.wait_ge(shifted, NG * (f + 1))
                    if g:
                        pe.wait_ge(sh_copied, 2 * (n - 1))
                    for w, bk in zip((ws1s, ws3s), SHARED[k]):
                        ins = pe.matmul(bank[bk][0:I, :], w[:, k * I:(k + 1) * I], XT[:, 512 * g:512 * g + 512],
                                        start=True, stop=True)
                    ins.then_inc(sh_ps, 1)

                def shared_out(g):
                    n = f * NSH + g
                    if n:
                        pe.wait_ge(z_added, n)
                    pe.matmul(bank[7][:, :], twice[:, :], X[:, 4 * g:4 * g + 4, :].rearrange("p i d -> p (i d)"),
                              start=True, stop=False, skip_group_check=True)
                    pe.wait_ge(sh_gated, 2 * n + 2)
                    for i in range(4):
                        for k in range(2):
                            ins = pe.matmul(bank[7][:, i * D:(i + 1) * D], HS[g % 2][k][:, i * P:(i + 1) * P], ws2s[:, k, :],
                                            start=False, stop=(k == 1), skip_group_check=True)
                    ins.then_inc(z_ps, 1)

                def base():
                    pe.wait_ge(totals, f + 1)
                    pe.matmul(bank[6][:, 0:NE], before[:, :], st2[:, 1, :], start=True, stop=True).then_inc(base_ps, 1)

                def look_up():
                    pe.wait_ge(sh_copied, 4 * (f + 1) * NSH)
                    for s in range(NS):
                        if s % (NS // NQT) == 0:
                            pe.wait_ge(table_ready, NQT * f + s // (NS // NQT) + 1)
                            pe.wait_ge(counts_ready, NQT * f + s // (NS // NQT) + 1)
                        for k in range(2):
                            e = 2 * s + k
                            ins = pe.matmul(bank[2 + s // PER][CAP * k:CAP * k + CAP, (s % PER) * RW:(s % PER + 1) * RW],
                                            OH[:, e, :], R[:, e, :], start=True, stop=True)
                        if s % PER == PER - 1 or s == NS - 1:
                            ins.then_inc(look_ps, 1)

                for g in range(NSH):
                    for k in range(2):
                        shared_hidden(g, k)
                    if g:
                        shared_out(g - 1)
                    if g == BASE_AFTER:
                        base()
                shared_out(NSH - 1)
                look_up()
                pe.wait_ge(z_added, (f + 1) * NSH)
                pe.wait_ge(slots_ready, NB * (f + 1))
                pe.wait_ge(w_in, 48 + 16 * f)

                def xb_turn(s):
                    pe.wait_ge(gathered[s % 8], 16 * (f * (NS // 8) + s // 8 + 1))
                    if s >= 2:
                        pe.wait_ge(xbT_sb, f * NS + s - 1)
                    pe.transpose(bank[(0, 5)[s % 2]][:, 0:P], A[:, s, :], ident[:, :]).then_inc(xbT_ps, 1)

                def hidden(s):
                    pe.wait_ge(xbT_sb, f * NS + s + 1)
                    if s >= 2:
                        pe.wait_ge(gated, f * NS + s - 1)
                    for w, off in ((w1s, 0), (w3s, I)):
                        for k in range(2):
                            ins = pe.matmul(bank[2 + s % 2][CAP * k:CAP * k + CAP, off:off + I], XBT[s % 2][:, CAP * k:CAP * k + CAP],
                                            w[:, 2 * s + k, :], start=True, stop=True)
                    ins.then_inc(h_ps, 1)

                def g_turn(s):
                    pe.wait_ge(gated, f * NS + s + 1)
                    if s >= 2:
                        pe.wait_ge(gT_sb, f * NS + s - 1)
                    pe.transpose(bank[(1, 6)[s % 2]][0:I, 0:P], GA[s % 2], ident[:, :]).then_inc(gT_ps, 1)

                def expert_out(s):
                    pe.wait_ge(gT_sb, f * NS + s + 1)
                    if s >= 2:
                        pe.wait_ge(y_sb, f * NS + s - 1)
                    for k in range(2):
                        ins = pe.matmul(bank[(4, 7)[s % 2]][CAP * k:CAP * k + CAP, 0:D], GT[s % 2][:, CAP * k:CAP * k + CAP],
                                        w2s[:, 2 * s + k, :], start=True, stop=True)
                    ins.then_inc(y_ps, 1)

                for s in range(NS + 3):
                    if s < NS:
                        xb_turn(s)
                    if 1 <= s <= NS:
                        hidden(s - 1)
                    if 2 <= s <= NS + 1:
                        g_turn(s - 2)
                    if s >= 3:
                        expert_out(s - 3)

            ffn(0)

            for g in range(NSH):
                xT(1, g)
            pe.wait_ge(xT_sb, 2 * NSH)
            for s in (v_ps, sc_ps, kv_ps, pr_ps, o_ps, anT_ps):
                pe.sem_inc(s, PRIMED)

            def project(b):
                pe.wait_ge(hTb_sb, b + 1)
                if not (isinstance(b, int) and b == 0):
                    pe.wait_ge(kv_sb, PRIMED + 2 * NQ * (b - 1))
                    pe.wait_ge(q_read, 2 * b)
                    pe.wait_ge(v_ready, b)
                    pe.wait_ge(k_read, 2 * b)
                pe.matmul(bank[0][:, :], wqkv[:, 0:D], HTB, start=True, stop=True).then_inc(qT_ps, 1)
                pe.matmul(bank[1][:, :], wqkv[:, D:2 * D], HTB, start=True, stop=True).then_inc(kT_ps, 1)
                for q in range(NQ):
                    ins = pe.matmul(bank[2][:, q * D:(q + 1) * D], HTB[:, q * P:(q + 1) * P], wqkv[:, 2 * D:3 * D],
                                    start=True, stop=True)
                ins.then_inc(v_ps, 1)

            def turn_k(b):
                if not (isinstance(b, int) and b == 0):
                    pe.wait_ge(oo_ready, PRIMED + b - 1)
                pe.wait_ge(k_ready, PRIMED + b + 1)
                for q in range(NQ):
                    ins = pe.transpose(bank[3][:, q * P:(q + 1) * P], KT[:, q * P:(q + 1) * P], ident[:, :])
                ins.then_inc(kn_ps, 1)

            def turn_out(b):
                if not (isinstance(b, int) and b == B - 1):
                    pe.wait_ge(kn_sb, PRIMED + b + 2)
                pe.wait_ge(an_ready, 2 * (b + 1))
                for c in range(NC):
                    ins = pe.transpose(bank[3][:, c * P:(c + 1) * P], AN[:, c, :], ident[:, :])
                ins.then_inc(anT_ps, 1)

            def project_out(b):
                pe.wait_ge(anT_sb, b + 1)
                for c in range(NC):
                    ins = pe.matmul(bank[3][:, c * D:(c + 1) * D], AT[:, c * P:(c + 1) * P], wout[:, :],
                                    start=True, stop=True)
                ins.then_inc(pr_ps, 1)

            def step(b, par, first=False, last=False):
                if not last:
                    project(b + 1)
                pe.wait_ge(q4_ready, 4 * b + 4)
                pe.wait_ge(k_ready, PRIMED + b + 1)
                if not first:
                    turn_out(b - 1)
                for g in range(4):
                    rows = slice(32 * g, 32 * g + 32)
                    for q in range(NQ):
                        for c in range(NC):
                            t0 = q * P + c * CHUNK
                            ins = pe.matmul(bank[4 + g][CHUNK * c:CHUNK * c + CHUNK, q * P:(q + 1) * P]
                                            .rearrange("p (j t) -> p j t", j=4),
                                            KT[rows, t0:t0 + CHUNK], Q4[rows, :, t0:t0 + CHUNK],
                                            start=True, stop=True)
                    ins.then_inc(sc_ps, 1)
                pe.wait_ge(kn_sb, PRIMED + b + 1)
                if last:
                    pe.wait_ge(v_ready, b + 1)
                else:
                    pe.wait_ge(q_read, 2 * (b + 2))
                    pe.wait_ge(v_ready, b + 2)
                for q in range(NQ):
                    if q == 1:
                        pe.wait_ge(sc_sb, 4 * b + 4)
                    if q >= 2:
                        pe.wait_ge(kv_sb, PRIMED + 2 * NQ * b + 2 * (q - 1))
                    for c in range(NC):
                        k = CHUNK * (c + 1)
                        ins = pe.matmul(bank[STATES[q % 2][c // 2]][:, (c % 2) * VW:(c % 2 + 1) * VW], KN[0:k, q, :],
                                        VN[par][0:k, q, :, :].rearrange("p h f -> p (h f)"), start=True, stop=True)
                    ins.then_inc(kv_ps, 1)
                if not first:
                    project_out(b - 1)
                pe.wait_ge(vx_ready, PRIMED + NC * (b + 1))
                pe.wait_ge(sc_sb, 4 * b + 4)
                for h in range(HEADS):
                    ob = bank[4 + h // 8][:, 0:NC * HV].rearrange("p (c h f) -> p c h f", c=NC, h=8)
                    for q in range(NQ):
                        o = (h // 4) * L + q * P + (h % 4) * CHUNK
                        pe.matmul(ob[32 * q:32 * q + 32, :, h % 8, :], PR[:, o:o + CHUNK],
                                  VX[:, q, h, :, :], start=(h % 8 == 0), stop=False, skip_group_check=True)
                pe.wait_ge(kv_sb, PRIMED + 2 * NQ * (b + 1))
                pe.wait_ge(sb_ready, PRIMED + NQ * (b + 1))
                for half in range(2):
                    for c in range(NC):
                        for q in range(NQ):
                            t0 = q * P + c * CHUNK
                            dst = bank[4 + half][32 * q:32 * q + 32, c * HV:(c + 1) * HV]
                            if q:
                                ins = pe.matmul(dst, QT[par][:, t0:t0 + CHUNK], SB[:, q, half * HV:(half + 1) * HV],
                                                start=False, stop=(c == 0), skip_group_check=True)
                            if c:
                                ins = pe.matmul(dst, QT[par][:, t0:t0 + CHUNK], SW[:, q, c - 1, half * HV:(half + 1) * HV],
                                                start=False, stop=True, skip_group_check=True)
                ins.then_inc(o_ps, 1)
                if not last:
                    turn_k(b + 1)

            project(0)
            turn_k(0)
            step(0, 0, first=True)
            with pe.Fori(0, (B - 2) // 2) as i:
                step(2 * i + 1, 1)
                step(2 * i + 2, 0)
            step(B - 1, 1, last=True)
            turn_out(B - 1)
            project_out(B - 1)

            ffn(1)

        @block.vector
        def _(dve):
            steps = [0]

            def then(ins):
                steps[0] += 1
                ins.then_inc(dve_step, 1)
                dve.wait_ge(dve_step, steps[0])

            def over(v, n):
                return v.unsqueeze(2).broadcast_to([P, v.shape[1], n])

            dve.memset(zeros[:, :], 0.0).then_inc(zero_set, 1)
            dve.memset(top8[:, :, :], 0.0)

            def norm(n):
                def update(g):
                    xg = X[:, GI * g:GI * g + GI, :].rearrange("p i d -> p (i d)")
                    cols = slice(g * GI * D, (g + 1) * GI * D)
                    if n == 0:
                        dve.wait_ge(part_in[g], 16)
                        return
                    if n == 2:
                        dve.wait_ge(attn_in, 16 * B)
                        then(dve.tensor_tensor(xg, xg, PL[:, cols], ALU.add))
                        return
                    dve.wait_ge(z_added, NSH * (1 + n // 2))
                    dve.wait_ge(part_in[g], 16 + 64 * (1 + n // 2))
                    for buf in PLANES:
                        then(dve.tensor_tensor(xg, xg, buf[:, cols], ALU.add))
                    dve.memset(st[:, 0, 0:1], 0.0).then_inc(group_ready, 1)

                def stats(g):
                    for i in range(GI * g, GI * g + GI):
                        ins = dve.bn_stats(bn[:, i, :], X[:, i, :])
                    then(ins)
                    for i in range(GI * g, GI * g + GI):
                        ins = dve.bn_aggr(mv[:, i, :], bn[:, i, :])
                    ins.then_inc(stats_ready, 1)

                def scales(g):
                    dve.wait_ge(std_ready, NG * n + g + 1)
                    cols = slice(GI * g, GI * g + GI)
                    then(dve.reciprocal(st[:, 4, cols], st[:, 3, cols]))
                    dve.scalar_tensor_tensor(st[:, 1, cols], mv[:, cols, 0], -1.0, st[:, 4, cols], ALU.mult, ALU.mult)\
                        .then_inc(scale_ready, 1)

                for g in range(NG):
                    update(g)
                    if n < 3:
                        stats(g)
                        if g:
                            scales(g - 1)
                if n < 3:
                    scales(NG - 1)

            def ffn(f):
                norm(2 * f)
                if f == 0:
                    dve.wait_ge(const_done, 1)
                    dve.wait_ge(small_in, 16 * N_SMALL)
                scores = R[:, :, NI:2 * NI].rearrange("p e i -> p i e")

                def shift(g):
                    dve.wait_ge(logits_ps, NG * f + g + 1)
                    lg = bank[2 + g][:, :].rearrange("p (i e) -> p i e", i=GI)
                    tiles = slice(GI * g, GI * g + GI)
                    then(dve.tensor_reduce(st[:, 5, tiles], lg, AX, ALU.max))
                    dve.tensor_tensor(EX[:, tiles, :], lg, over(st[:, 5, tiles], NE), ALU.subtract).then_inc(shifted, 1)

                def total(g):
                    dve.wait_ge(exp_done, NG * f + g + 1)
                    tiles = slice(GI * g, GI * g + GI)
                    then(dve.tensor_reduce(st[:, 6, tiles], EX[:, tiles, :], AX, ALU.add))
                    dve.reciprocal(st[:, 7, tiles], st[:, 6, tiles]).then_inc(recip_ready, 1)

                def top(g):
                    dve.wait_ge(scores_ready, NG * f + g + 1)
                    tiles = slice(GI * g, GI * g + GI)
                    then(dve.tensor_tensor(BI[:, tiles, 0:NE], scores[:, tiles, :],
                                           gateb[:, :].unsqueeze(1).broadcast_to([P, GI, NE]), ALU.add))
                    for i in range(GI * g, GI * g + GI):
                        ins = dve.max(top8[:, i, :], BI[:, i, 0:NE])
                    then(ins)
                    dve.memset(top8[:, tiles, TOPK:TOPK + 1], -1e30)
                    then(dve.memset(top8[:, tiles, TOPK + 1:TOPK + 2], -2e30))
                    for i in range(GI * g, GI * g + GI):
                        ins = dve.match_replace(RP[:, i, :], top8[:, i, :], BI[:, i, :], -3e30)
                    return ins

                dve.memset(BI[:, :, NE:NE + 1], -1e30)
                dve.memset(BI[:, :, NE + 1:NE + 2], -2e30)
                shift(0)
                shift(1)
                total(0)
                shift(2)
                total(1)
                shift(3)
                total(2)
                top(0)
                total(3)
                for g in range(1, NG):
                    ins = top(g)
                then(ins)
                then(dve.tensor_tensor(M.rearrange("p e i -> p i e"), RP[:, :, 0:NE], BI[:, :, 0:NE], ALU.not_equal))
                dve.wait_ge(rows_out, 16 * NG * (f + 1))
                dve.wait_ge(xT_ps, (2 * f + 1) * NSH)
                then(dve.tensor_tensor_scan(A_flat[:, 0:NE * NI], Eb[:, :], Eb[:, :], 0.0, ALU.add, ALU.max))
                dve.memset(st2[:, 0, 0:1], 0.0)
                then(dve.tensor_copy(st2[:, 0, 1:NE], CUM[:, 0:NE - 1, NI - 1]))
                dve.tensor_tensor(st2[:, 1, :], CUM[:, :, NI - 1], st2[:, 0, :], ALU.subtract).then_inc(totals, 1)
                dve.wait_ge(base_ps, f + 1)
                then(dve.tensor_copy(st2[:, 2, :], bank[6][:, 0:NE]))
                then(dve.tensor_tensor(st2[:, 3, :], st2[:, 2, :], st2[:, 1, :], ALU.add))
                dve.tensor_tensor(st2[:, 4, :], st2[:, 2, :], st2[:, 0, :], ALU.subtract).then_inc(base_ready, 1)
                dve.tensor_scalar(R[:, :, 2 * NI], st2[:, 0, :], 0.0, tok0[:, 0:1], ALU.mult, ALU.add)
                then(dve.tensor_scalar(bnd[:, :, :], st2[:, 2:4, :], float(CAP), None, ALU.min))
                for h in range(NQT):
                    ex = slice(HE * h, HE * h + HE)
                    c_h = slot_ce[:, :, ex]
                    ge, lt = GL[h % 2]
                    if h >= 2:
                        dve.wait_ge(table_ready, NQT * f + h - 1)
                    dve.tensor_tensor(ge, c_h, bnd[:, 0:1, ex].broadcast_to([P, CAP, HE]), ALU.is_ge)
                    then(dve.tensor_tensor(lt, c_h, bnd[:, 1:2, ex].broadcast_to([P, CAP, HE]), ALU.is_lt))
                    dve.tensor_tensor(OH[:, ex, :].rearrange("p e c -> p c e"), ge, lt, ALU.mult).then_inc(table_ready, 1)
                for b in range(NB):
                    ss = slice(PER * b, min(PER * b + PER, NS))
                    n = ss.stop - ss.start
                    dve.wait_ge(look_ps, NB * f + b + 1)
                    bk = bank[2 + b][:, 0:n * RW].rearrange("p (s r) -> p s r", s=n)
                    then(dve.tensor_scalar(LE[:, ss, :], bk[:, :, 0:NI], c_of_p[:, 0:1], None, ALU.is_le))
                    then(dve.tensor_reduce(sl[:, 0, ss], LE[:, ss, :], AX, ALU.add))
                    dve.scalar_tensor_tensor(sl[:, 1, ss], sl[:, 0, ss], -NONE, bk[:, :, 2 * NI], ALU.add, ALU.add)
                    then(dve.tensor_tensor(LE[:, ss, :], col_i[:, :].unsqueeze(1).broadcast_to([P, n, NI]),
                                           over(sl[:, 0, ss], NI), ALU.is_equal))
                    dve.tensor_copy(tok_i[:, ss], sl[:, 1, ss])
                    dve.tensor_tensor(put_i[:, ss], sl[:, 1, ss], plane0[:, ss], ALU.add)
                    then(dve.tensor_tensor(LE[:, ss, :], LE[:, ss, :], bk[:, :, NI:2 * NI], ALU.mult))
                    dve.tensor_reduce(sl[:, 2, ss], LE[:, ss, :], AX, ALU.add).then_inc(slots_ready, 1)
                dve.wait_ge(slots_ready, NB * (f + 1))

                def gate(s):
                    dve.wait_ge(silu_done, f * NS + s + 1)
                    if s >= 2:
                        dve.wait_ge(gT_ps, f * NS + s - 1)
                    dve.tensor_tensor(GA[s % 2], SG[s % 2], bank[2 + s % 2][:, I:2 * I], ALU.mult).then_inc(gated, 1)

                def weigh(s):
                    dve.wait_ge(y_ps, f * NS + s + 1)
                    dve.tensor_scalar(Y[:, s, :], bank[(4, 7)[s % 2]][:, 0:D], sl[:, 2, s:s + 1], 0.5,
                                      ALU.mult, ALU.mult).then_inc(y_sb, 1)

                for s in range(NS + 3):
                    if 1 <= s <= NS:
                        gate(s - 1)
                    if s >= 3:
                        weigh(s - 3)
            ffn(0)

            norm(1)
            for v in VN:
                then(dve.memset(v, 1.0))
            then(dve.memset(SB[:, 0, :], 0.0))
            for s in (q_ready, k_ready, kv_sb, oo_ready, sb_ready):
                dve.sem_inc(s, PRIMED)

            def feature(b, k, e, r, dst, last_readers):
                dve.wait_ge((q_read, k_read)[k], 2 * (b + 1))
                dve.tensor_scalar(e, e, 1.0, FEAT_EPS, ALU.min, ALU.add).then_inc(phi_step, 1)
                dve.wait_ge(phi_step, 2 * b + k + 1)
                dve.wait_ge(*last_readers)
                dve.tensor_tensor(dst, e, r, ALU.add).then_inc((q_ready, k_ready)[k], 1)

            def value(b, par):
                dve.wait_ge(v_ps, PRIMED + b + 1)
                if not (isinstance(b, int) and b < 2):
                    dve.wait_ge(vx_ready, PRIMED + NC * (b - 1))
                    dve.wait_ge(kv_ps, PRIMED + NQ * (b - 1))
                dve.tensor_tensor(VN[par][:, :, :, 0:E],
                                  bank[2][:, :].rearrange("p (q h f) -> p q h f", q=NQ, h=HEADS),
                                  bv[:, :].rearrange("p (h f) -> p h f", h=HEADS).unsqueeze(1)
                                  .broadcast_to([P, NQ, HEADS, E]), ALU.add).then_inc(v_ready, 1)

            def q_feature(b, par):
                n = PRIMED if isinstance(b, int) and b < 2 else PRIMED + b - 1
                feature(b, 0, EQ, RQ, QT[par], (o_ps, n))

            def k_feature(b):
                feature(b, 1, EK, RK, KT, (sc_ps, PRIMED + 4 * b))

            def project_bias(b):
                dve.wait_ge(pr_ps, PRIMED + b + 1)
                dve.wait_ge(oo_stored, PRIMED + b)
                dve.tensor_tensor(OO.rearrange("p (c d) -> p c d", c=NC),
                                  bank[3][:, :].rearrange("p (c d) -> p c d", c=NC),
                                  bo[:, :].unsqueeze(1).broadcast_to([P, NC, D]), ALU.add).then_inc(oo_ready, 1)

            def step(b, par, first=False, last=False):
                if not last:
                    value(b + 1, 1 - par)
                    q_feature(b + 1, 1 - par)
                for g in range(4):
                    dve.wait_ge(sc_ps, PRIMED + 4 * b + g + 1)
                    if g == 0:
                        dve.wait_ge(o_ps, PRIMED + b)
                    dve.tensor_tensor(PR[:, g * L:(g + 1) * L].rearrange("p (n t) -> p n t", t=CHUNK),
                                      bank[4 + g][:, :].rearrange("p (n t) -> p n t", t=CHUNK),
                                      causal[:, :].unsqueeze(1).broadcast_to([P, L // CHUNK, CHUNK]),
                                      ALU.mult).then_inc(sc_sb, 1)
                for q in range(NQ):
                    dve.wait_ge(kv_ps, PRIMED + NQ * b + q + 1)
                    for k in range(2):
                        dve.tensor_tensor(SW[:, q, 2 * k:2 * k + 2, :],
                                          bank[STATES[q % 2][k]][:, 0:2 * VW].rearrange("p (c v) -> p c v", c=2),
                                          own[:, :].unsqueeze(1).broadcast_to([P, 2, VW]), ALU.mult).then_inc(kv_sb, 1)
                    dve.wait_ge(kv_sb, PRIMED + 2 * NQ * b + 2 * q + 2)
                    dve.wait_ge(sb_ready, PRIMED + NQ * b + q)
                    if q < NQ - 1:
                        dve.tensor_tensor(SB[:, q + 1, :], SB[:, q, :], SW[:, q, NC - 1, :], ALU.add).then_inc(sb_ready, 1)
                    else:
                        dve.memset(st[:, 0, 0:1], 0.0).then_inc(sb_ready, 1)
                if not last:
                    k_feature(b + 1)
                if not first:
                    project_bias(b - 1)
                dve.wait_ge(o_ps, PRIMED + b + 1)
                if not first:
                    dve.wait_ge(anT_ps, PRIMED + b)
                for k in range(2):
                    ob = bank[4 + k][:, 0:NC * HV].rearrange("p (n f) -> p n f", f=E + 1)
                    den = top8[:, 8 * k:8 * k + 4, :].rearrange("p a b -> p (a b)")
                    rec = top8[:, 8 * k + 4:8 * k + 8, :].rearrange("p a b -> p (a b)")
                    dve.tensor_scalar(den, ob[:, :, E], DEN_EPS, None, ALU.add).then_inc(o_step, 1)
                    dve.wait_ge(o_step, 4 * b + 2 * k + 1)
                    dve.reciprocal(rec, den).then_inc(o_step, 1)
                    dve.wait_ge(o_step, 4 * b + 2 * k + 2)
                    dve.tensor_tensor(AN[:, :, k * 8 * E:(k + 1) * 8 * E].rearrange("p c (h f) -> p c h f", h=8),
                                      bank[4 + k][:, 0:NC * HV].rearrange("p (c h f) -> p c h f", c=NC, h=8)[:, :, :, 0:E],
                                      rec.rearrange("p (c h) -> p c h", c=NC).unsqueeze(3)
                                      .broadcast_to([P, NC, 8, E]), ALU.mult).then_inc(an_ready, 1)

            value(0, 0)
            q_feature(0, 0)
            k_feature(0)
            step(0, 0, first=True)
            with dve.Fori(0, (B - 2) // 2) as i:
                step(2 * i + 1, 1)
                step(2 * i + 2, 0)
            step(B - 1, 1, last=True)
            project_bias(B - 1)

            ffn(1)
            norm(3)


def kernel(**inputs):
    import numpy as _np
    import concourse.bacc as _bacc
    from concourse import mybir as _mybir
    from concourse.bass_utils import run_bass_kernel_spmd as _run

    a = {k: _np.asarray(v) for k, v in inputs.items()}
    inner = a["L0_ffn_w1"].shape[1]
    laid = {
        "x": a["L0_attn_x"],
        "w_qkv": a["L0_attn_W_qkv"],
        "b_qkv": a["L0_attn_b_qkv"],
        "w_out": a["L0_attn_W_out"],
        "b_out": a["L0_attn_b_out"],
        "gate_wT": a["L0_ffn_gate_w"].T,
        "gate_b": a["L0_ffn_gate_b"],
        "w1T": a["L0_ffn_w1"].transpose(2, 0, 1),
        "w2T": a["L0_ffn_w2"].transpose(2, 0, 1),
        "w3T": a["L0_ffn_w3"].transpose(2, 0, 1),
        "ws1T": a["L0_ffn_ws1"].T,
        "ws2T": a["L0_ffn_ws2"].T.reshape(2, inner, -1).transpose(1, 0, 2),
        "ws3T": a["L0_ffn_ws3"].T,
    }
    nc = _bacc.Bacc("TRN2", target_bir_lowering=False, num_devices=1)
    arrays, args = {}, []
    for name, v in laid.items():
        v = _np.ascontiguousarray(v)
        arrays[f"in_{name}"] = v
        args.append(nc.dram_tensor(f"in_{name}", v.shape, _mybir.dt.from_np(v.dtype), kind="ExternalInput").ap())
    out = nc.dram_tensor("out_x", laid["x"].shape, _mybir.dt.from_np(laid["x"].dtype), kind="ExternalOutput").ap()
    macaron_kernel(nc, *args, out)
    r = _run(nc, [arrays], core_ids=[0])
    return r.results[0]["out_x"]
```

```python
from contextlib import ExitStack

import concourse.bass as bass
from concourse import mybir

ALU = mybir.AluOpType
ACT = mybir.ActivationFunctionType
AX = mybir.AxisListType.X
F32 = mybir.dt.float32
BF16 = mybir.dt.bfloat16
I32 = mybir.dt.int32

P = 128
TOPK = 6
CAP = 64
LN_EPS = 1e-5
FEAT_EPS = 1e-4
DEN_EPS = 1e-6
HEADS = 16
CHUNK = 32
NONE = -32768.0


def macaron_kernel(nc, x, w_qkv, b_qkv, w_out, b_out, gate_wT, gate_b, w1T, w2T, w3T, ws1T, ws2T, ws3T, out):
    B, L, D = x.shape
    T = B * L
    NI = T // P
    NE = gate_wT.shape[1]
    I = w1T.shape[2]
    NS = NE * CAP // P
    E = D // HEADS
    VW = HEADS * (E + 1)
    HV = VW // 2
    NQ = L // P
    NC = P // CHUNK
    RW = 2 * NI + 1
    PER = 7
    NB = -(-NS // PER)
    LEAD = (16, 6)
    NQT = 4
    NG = 4
    GI = NI // NG
    NSH = NI // 4
    EARLY = 4
    BASE_AFTER = EARLY - 2
    QS = float(E) ** -0.5
    NH = 2 * NQ
    STATES = (0, 2, 1)
    AFTER = ((), (0, 1, 2), (3, 4), (5, 6, 7))

    ctx = ExitStack()
    with ctx:
        def sb(name, shape, dt=F32):
            return ctx.enter_context(nc.sbuf_tensor(name, shape, dt))

        def sem(name):
            return ctx.enter_context(nc.semaphore(name))

        rows_d = nc.dram_tensor("rows_d", (T, D), F32, kind="Internal").ap()
        planes_d = [nc.dram_tensor(f"planes{f}_d", (4 * T, D), F32, kind="Internal").ap() for f in range(2)]
        attn_d = nc.dram_tensor("attn_d", (T, D), F32, kind="Internal").ap()

        X = sb("X", [P, NI, D])
        A = sb("A", [P, NI, D])
        XT = sb("XT", [P, T])
        Bb = sb("Bb", [P, NE * RW])
        Cb = sb("Cb", [P, 2 * NI * (NE + 2)])
        Eb = sb("Eb", [P, NE * NI])
        w1s = sb("w1s", [P, NE, I])
        w3s = sb("w3s", [P, NE, I])
        w2s = sb("w2s", [I, NE, D])
        ring = sb("ring", [P, 2 * (P + I + I + P)])
        ident = sb("ident", [P, P])
        before = sb("before", [P, P])
        causal = sb("causal", [P, CHUNK])
        own = sb("own", [P, VW])
        chm = sb("chm", [P, NC])
        upto = sb("upto", [P, NC])
        hm = sb("hm", [P, 4])
        col_i = sb("col_i", [P, NI])
        c_of_p = sb("c_of_p", [P, 1])
        tok0 = sb("tok0", [P, 1])
        plane0 = sb("plane0", [P, NS])
        twice = sb("twice", [P, P])
        gate_s = sb("gate_s", [P, NE])
        gateb = sb("gateb", [P, NE])
        ws1s = sb("ws1s", [P, 2 * I])
        ws3s = sb("ws3s", [P, 2 * I])
        ws2s = sb("ws2s", [I, 2, D])
        wqkv = sb("wqkv", [P, 3 * D])
        wout = sb("wout", [P, D])
        bq = sb("bq", [P, 3])
        bv = sb("bv", [P, D])
        bo = sb("bo", [P, D])
        st = sb("st", [P, 8, NI])
        top8 = sb("top8", [P, NI, 8])
        st2 = sb("st2", [P, 5, NE])
        sl = sb("sl", [P, 3, NS])
        tok_i = sb("tok_i", [P, NS], I32)
        put_i = sb("put_i", [P, NS], I32)
        eps = sb("eps", [P, 1])
        zeros = sb("zeros", [P, 4 * D])
        PL = sb("PL", [P, NI * D])
        slot_ce = sb("slot_ce", [P, CAP, NE], BF16)
        bnd = sb("bnd", [P, 2, NE], BF16)
        bn = sb("bn", [P, NI, 6])
        mv = sb("mv", [P, NI, 2])

        A_flat = A[:, :, :].rearrange("p i d -> p (i d)")
        R = Bb[:, :].rearrange("p (e r) -> p e r", e=NE)
        Y = Bb[:, 0:NS * D].rearrange("p (s d) -> p s d", s=NS)
        BI = Cb[:, 0:NI * (NE + 2)].rearrange("p (i e) -> p i e", i=NI)
        RP = Cb[:, NI * (NE + 2):2 * NI * (NE + 2)].rearrange("p (i e) -> p i e", i=NI)
        OH = Cb[:, 0:NE * CAP].rearrange("p (e c) -> p e c", e=NE)
        HE = NE // NQT
        GL = [[A_flat[:, 2048 + 512 * (2 * j + k):2560 + 512 * (2 * j + k)].bitcast(BF16)
               .rearrange("p (c e) -> p c e", c=CAP) for k in range(2)] for j in range(2)]
        EX = Eb[:, :].rearrange("p (i e) -> p i e", i=NI)
        M = Eb[:, :].rearrange("p (e i) -> p e i", e=NE)
        CUM = A_flat[:, 0:NE * NI].rearrange("p (e i) -> p e i", e=NE)
        LE = Eb[:, 0:NS * NI].rearrange("p (s i) -> p s i", s=NS)
        XBT = [ring[:, k * P:(k + 1) * P] for k in range(2)]
        o = 2 * P
        SG = [ring[:, o + k * I:o + (k + 1) * I] for k in range(2)]
        o += 2 * I
        GA = [ring[:, o + k * I:o + (k + 1) * I] for k in range(2)]
        o += 2 * I
        GT = [ring[0:I, o + k * P:o + (k + 1) * P] for k in range(2)]

        SHARED_BUFS = []
        for buf in (PL, w3s[:, :, :].rearrange("p e i -> p (e i)")):
            parts = [buf[0:I, 512 * k:512 * k + 512] for k in range(8)]
            SHARED_BUFS.append((parts[0:2], parts[2:4], (parts[4:6], parts[6:8])))

        PR = A_flat[:, 0:4 * L]
        Q4 = A_flat[:, 4 * L:8 * L].rearrange("p (j t) -> p j t", j=4)
        VX = Bb[:, 0:NQ * NC * VW].rearrange("p (q h c f) -> p q h c f", q=NQ, h=HEADS, c=NC)
        o = NQ * NC * VW
        HTB, KT, QT0 = (Bb[:, o + k * L:o + (k + 1) * L] for k in range(3))
        SW = Cb[:, 0:NQ * NC * VW].rearrange("p (q c v) -> p q c v", q=NQ, c=NC)
        VN0 = Cb[:, o:o + NQ * VW]
        o += NQ * VW
        EQ, RQ, AT, OO = (Eb[:, k * L:(k + 1) * L] for k in range(4))
        spare = w3s[:, :, :].rearrange("p e i -> p (e i)")
        QT1, EK, RK = (spare[:, k * L:(k + 1) * L] for k in range(3))
        QT = (QT0, QT1)
        VN = [v.rearrange("p (q h f) -> p q h f", q=NQ, h=HEADS) for v in (VN0, spare[:, 3 * L:3 * L + NQ * VW])]
        KN = spare[:, 4 * L + NQ * VW:4 * L + NQ * VW + NC * L].rearrange("p (c q k) -> p c q k", c=NC, q=NQ)
        AN = ring[:, 0:L].rearrange("p (c k) -> p c k", c=NC)

        bank = [ctx.enter_context(nc.psum_tensor(f"bank{k}", [P, 512], F32)) for k in range(8)]

        part_in = [sem(f"part_in{g}") for g in range(NG)]
        small_in = sem("small_in")
        stats_ready = sem("stats_ready")
        scale_ready = sem("scale_ready")
        recip_ready = sem("recip_ready")
        scores_ready = sem("scores_ready")
        biased = sem("biased")
        base_ready = sem("base_ready")
        counts_ready = sem("counts_ready")
        sh_copied = sem("sh_copied")
        group_ready = sem("group_ready")
        w_in = sem("w_in")
        zero_set = sem("zero_set")
        planes_zero = sem("planes_zero")
        const_step = sem("const_step")
        ident_ready = sem("ident_ready")
        const_done = sem("const_done")
        dve_step = sem("dve_step")
        std_ready = sem("std_ready")
        normed = [sem(f"normed{g}") for g in range(NG)]
        xT_ps = sem("xT_ps")
        xT_sb = sem("xT_sb")
        rows_out = sem("rows_out")
        logits_ps = sem("logits_ps")
        shifted = sem("shifted")
        exp_done = sem("exp_done")
        totals = sem("totals")
        base_ps = sem("base_ps")
        table_ready = sem("table_ready")
        look_ps = sem("look_ps")
        tokens_ready = sem("tokens_ready")
        slots_ready = sem("slots_ready")
        gathered = [sem(f"gathered{k}") for k in range(8)]
        xbT_ps = sem("xbT_ps")
        xbT_sb = sem("xbT_sb")
        h_ps = sem("h_ps")
        silu_done = sem("silu_done")
        gated = sem("gated")
        gT_ps = sem("gT_ps")
        gT_sb = sem("gT_sb")
        y_ps = sem("y_ps")
        y_sb = sem("y_sb")
        added = [sem(f"added{k}") for k in range(2)]
        sh_ps = sem("sh_ps")
        sh_gated = sem("sh_gated")
        z_ps = sem("z_ps")
        z_added = sem("z_added")
        planes_added = sem("planes_added")
        out_done = sem("out_done")
        PRIMED = 1
        hTb_sb = sem("hTb_sb")
        qT_ps = sem("qT_ps")
        kT_ps = sem("kT_ps")
        v_ps = sem("v_ps")
        bq_scaled = sem("bq_scaled")
        q_read = sem("q_read")
        k_read = sem("k_read")
        phi_step = sem("phi_step")
        q_ready = sem("q_ready")
        k_ready = sem("k_ready")
        q4_ready = sem("q4_ready")
        v_ready = sem("v_ready")
        vx_ready = sem("vx_ready")
        kn_ps = sem("kn_ps")
        kn_sb = sem("kn_sb")
        sc_ps = sem("sc_ps")
        sc_sb = sem("sc_sb")
        kv_ps = sem("kv_ps")
        kv_sb = sem("kv_sb")
        sb_ready = sem("sb_ready")
        o_ps = sem("o_ps")
        o_step = sem("o_step")
        an_ready = sem("an_ready")
        anT_ps = sem("anT_ps")
        anT_sb = sem("anT_sb")
        pr_ps = sem("pr_ps")
        oo_ready = sem("oo_ready")
        attn_out = sem("attn_out")
        oo_stored = sem("oo_stored")
        attn_in = [sem(f"attn_in{g}") for g in range(NG)]

        x_blk = x.rearrange("b l d -> (b l) d").rearrange("(p i) d -> p i d", p=P)
        out_blk = out.rearrange("b l d -> (b l) d").rearrange("(p i) d -> p i d", p=P)
        rows_blk = rows_d.rearrange("(p i) d -> p i d", p=P)
        PLANES = (A_flat, PL[:, :], Cb[:, 0:T], Bb[:, 0:T])
        N_SMALL = 12

        SHARED = ((0, 1), (4, 5))
        block = ctx.enter_context(nc.Block())

        @block.sync
        def _(sp):
            for g in range(NG):
                sp.dma_start(X[:, GI * g:GI * g + GI, :], x_blk[:, GI * g:GI * g + GI, :]).then_inc(part_in[g], 16)
            sp.dma_start(gate_s[:, :], gate_wT).then_inc(small_in, 16)
            sp.dma_start(gateb[:, :], gate_b.rearrange("(a e) -> a e", a=1).broadcast_to([P, NE])).then_inc(small_in, 16)
            sp.dma_start(ws1s[:, :], ws1T).then_inc(small_in, 16)
            sp.dma_start(ws3s[:, :], ws3T).then_inc(small_in, 16)
            sp.dma_start(ws2s[:, :, :], ws2T).then_inc(small_in, 16)
            sp.dma_start(wqkv[:, :], w_qkv).then_inc(small_in, 16)
            sp.dma_start(wout[:, :], w_out).then_inc(small_in, 16)
            sp.dma_start(bq[:, 0:1], b_qkv[0:D].rearrange("(p a) -> p a", a=1)).then_inc(small_in, 16)
            sp.dma_start(bq[:, 1:2], b_qkv[D:2 * D].rearrange("(p a) -> p a", a=1)).then_inc(small_in, 16)
            sp.dma_start(bq[:, 2:3], b_qkv[0:D].rearrange("(p a) -> p a", a=1)).then_inc(small_in, 16)
            sp.dma_start(bv[:, :], b_qkv[2 * D:3 * D].rearrange("(a e) -> a e", a=1).broadcast_to([P, D])).then_inc(small_in, 16)
            sp.dma_start(bo[:, :], b_out.rearrange("(a e) -> a e", a=1).broadcast_to([P, D])).then_inc(small_in, 16)
            def clear_planes(f):
                for k in range(4):
                    dst = planes_d[f][k * T:(k + 1) * T, :].rearrange("(p a i) d -> p a (i d)", p=P, i=4)
                    sp.dma_start(dst, zeros[:, :].unsqueeze(1).broadcast_to([P, NI // 4, 4 * D])).then_inc(planes_zero, 16)

            for dst, src in ((w1s, w1T), (w3s, w3T), (w2s, w2T)):
                sp.dma_start(dst[:, :, :], src).then_inc(w_in, 16)

            for f in range(2):
                for g in range(NG):
                    sp.wait_ge(normed[g], 2 * f + 1)
                    sp.dma_start(rows_blk[:, GI * g:GI * g + GI, :], A[:, GI * g:GI * g + GI, :]).then_inc(rows_out, 16)
                if f == 0:
                    sp.wait_ge(zero_set, 1)
                    clear_planes(0)
                for k in range(2):
                    sp.wait_ge(added[k], 16 * (NS // 2) * (f + 1))
                sp.wait_ge(z_added, NSH * f + EARLY)
                for g in range(NG):
                    cols = slice(g * GI * D, (g + 1) * GI * D)
                    for k, buf in enumerate(PLANES):
                        src = planes_d[f][k * T:(k + 1) * T, :].rearrange("(p i) d -> p (i d)", p=P)
                        sp.dma_start(buf[:, cols], src[:, cols]).then_inc(part_in[g], 16)
                if f == 0:
                    clear_planes(1)
                    sp.sem_inc(oo_stored, PRIMED)
                    for b in range(B):
                        sp.wait_ge(oo_ready, PRIMED + b + 1)
                        for q in range(NQ):
                            sp.dma_start(attn_d[b * L + q * P:b * L + (q + 1) * P, :].rearrange("(c t) d -> t c d", t=CHUNK),
                                         OO[32 * q:32 * q + 32, :].rearrange("p (c d) -> p c d", c=NC)).then_inc(attn_out, 16)
                        sp.wait_ge(attn_out, 16 * NQ * (b + 1))
                        sp.sem_inc(oo_stored, 1)
                        rows = slice(P // B * b, P // B * (b + 1))
                        sp.wait_ge(group_ready, NG)
                        for g in range(NG):
                            cols = slice(g * GI * D, (g + 1) * GI * D)
                            sp.dma_start(PL[rows, cols], attn_d[b * L:(b + 1) * L, :].rearrange("(p i) d -> p (i d)", p=P // B)
                                         [:, cols]).then_inc(attn_in[g], 16)
                    sp.dma_start(w3s[:, :, :], w3T).then_inc(w_in, 16)
            for g in range(NG):
                sp.wait_ge(group_ready, NG + g + 1)
                sp.dma_start(out_blk[:, GI * g:GI * g + GI, :], X[:, GI * g:GI * g + GI, :]).then_inc(out_done, 16)
            sp.wait_ge(out_done, 16 * NG)
            sp.wait_ge(planes_zero, 16 * 8)

        @block.gpsimd
        def _(pool):
            made = [0]

            def then(ins):
                made[0] += 1
                ins.then_inc(const_step, 1)
                pool.wait_ge(const_step, made[0])

            def keep(t, op, base, pattern, per_partition, fill):
                then(pool.affine_select(out=t, in_=t, compare_op=op, fill=fill, base=base, pattern=pattern,
                                        channel_multiplier=per_partition))

            def count(t, base, pattern, per_partition):
                then(pool.iota(t, pattern=pattern, base=base, channel_multiplier=per_partition,
                               allow_small_or_imprecise_dtypes=True))

            then(pool.memset(ident[:, :], 0.0))
            keep(ident[:, :], ALU.not_equal, 0, [[-1, P]], 1, 1.0)
            pool.memset(eps[:, :], LN_EPS).then_inc(ident_ready, 1)
            then(pool.memset(twice[:, :], 0.0))
            keep(twice[:, :], ALU.not_equal, 0, [[-1, P]], 1, 2.0)
            then(pool.memset(before[:, :], 1.0))
            keep(before[:, :], ALU.is_gt, 0, [[1, P]], -1, 0.0)
            then(pool.memset(causal[:, :], 1.0))
            for c in range(NC):
                keep(causal[CHUNK * c:CHUNK * c + CHUNK, :], ALU.is_ge, 0, [[1, CHUNK]], -1, 0.0)
            then(pool.memset(own[:, :], 1.0))
            ov = own[:, :].rearrange("p (h f) -> p h f", h=HEADS)
            keep(ov, ALU.is_ge, 0, [[-E, HEADS], [0, E + 1]], 1, 0.0)
            keep(ov, ALU.is_ge, E - 1, [[E, HEADS], [0, E + 1]], -1, 0.0)
            then(pool.memset(chm[:, :], 1.0))
            keep(chm[:, :], ALU.is_ge, 0, [[-CHUNK, NC]], 1, 0.0)
            keep(chm[:, :], ALU.is_ge, CHUNK - 1, [[CHUNK, NC]], -1, 0.0)
            then(pool.memset(upto[:, :], 1.0))
            keep(upto[:, :], ALU.is_ge, CHUNK - 1, [[CHUNK, NC]], -1, 0.0)
            own3 = own[:, :].rearrange("p (g j f) -> p j g f", g=4, j=4)
            then(pool.tensor_tensor(out=hm[:, :], in0=own3[:, :, 0, 0], in1=own3[:, :, 1, 0], op=ALU.add))
            for k in (2, 3):
                then(pool.tensor_tensor(out=hm[:, :], in0=hm[:, :], in1=own3[:, :, k, 0], op=ALU.add))
            count(col_i[:, :], 0, [[1, NI]], 0)
            for k in range(2):
                count(c_of_p[k * CAP:(k + 1) * CAP, :], 0, [[0, 1]], 1)
                count(plane0[k * CAP:(k + 1) * CAP, :], k * T, [[0, NS // 2], [2 * T, 2]], 0)
            count(tok0[:, :], int(NONE), [[0, 1]], NI)
            count(slot_ce[:, :, :], 0, [[1, CAP], [0, NE]], 0)
            pool.memset(st2[:, 0, :], 0.0).then_inc(const_done, 1)

            for f in range(2):
                pool.wait_ge(small_in, 16 * N_SMALL)
                for g in range(NG):
                    pool.wait_ge(recip_ready, NG * f + g + 1)
                    tiles = slice(GI * g, GI * g + GI)
                    pool.tensor_tensor(out=R[:, :, NI:2 * NI].rearrange("p e i -> p i e")[:, tiles, :], in0=EX[:, tiles, :],
                                       in1=st[:, 7, tiles].unsqueeze(2).broadcast_to([P, GI, NE]),
                                       op=ALU.mult).then_inc(scores_ready, 1)
                    pool.wait_ge(scores_ready, NG * f + g + 1)
                    pool.tensor_tensor(out=BI[:, tiles, 0:NE], in0=R[:, :, NI:2 * NI].rearrange("p e i -> p i e")[:, tiles, :],
                                       in1=gateb[:, :].unsqueeze(1).broadcast_to([P, GI, NE]), op=ALU.add)\
                        .then_inc(biased, 1)

                def counts():
                    for h in range(NQT):
                        ex = slice(HE * h, HE * h + HE)
                        pool.wait_ge(base_ready, f + 1)
                        pool.tensor_tensor(out=R[:, ex, 0:NI], in0=CUM[:, ex, :],
                                           in1=st2[:, 4, ex].unsqueeze(2).broadcast_to([P, HE, NI]),
                                           op=ALU.add).then_inc(counts_ready, 1)

                def shared_gates(g):
                    SH, H3, HS = SHARED_BUFS[g >= EARLY]
                    for k in range(2):
                        n = (f * NSH + g) * 2 + k
                        pool.wait_ge(sh_copied, 2 * n + 2)
                        if g >= 2:
                            pool.wait_ge(z_ps, f * NSH + g - 1)
                        pool.tensor_tensor(out=HS[g % 2][k], in0=SH[k], in1=H3[k], op=ALU.mult).then_inc(sh_gated, 1)

                for g in range(EARLY):
                    shared_gates(g)
                    if g == BASE_AFTER:
                        counts()
                pool.wait_ge(counts_ready, NQT * (f + 1))
                pool.wait_ge(rows_out, 16 * NG * (f + 1))

                def add(s):
                    if s == 0:
                        pool.wait_ge(planes_zero, 16 * 4 * (f + 1))
                    pool.wait_ge(y_sb, f * NS + s + 1)
                    n = f * (NS // 2) + s // 2
                    if n:
                        pool.wait_ge(added[s % 2], 16 * n)
                    pool.indirect_dma_start(out=planes_d[f], in_=Y[:, s, :], in_offset=None,
                                            out_offset=bass.IndirectOffsetOnAxis(ap=put_i[:, s:s + 1], axis=0),
                                            bounds_check=4 * T - 1, oob_is_err=False,
                                            compute_op=ALU.add).then_inc(added[s % 2], 16)

                fetched = 0
                for s in range(NS):
                    ahead = min(NS, s + 1 + max(LEAD[1], LEAD[0] - s // 2))
                    for t in range(fetched, ahead):
                        pool.wait_ge(tokens_ready, NB * f + t // PER + 1)
                        n = f * (NS // 8) + t // 8
                        if n:
                            pool.wait_ge(gathered[t % 8], 16 * n)
                        pool.indirect_dma_start(out=A[:, t, :], out_offset=None, in_=rows_d,
                                                in_offset=bass.IndirectOffsetOnAxis(ap=tok_i[:, t:t + 1], axis=0),
                                                bounds_check=T - 1, oob_is_err=False).then_inc(gathered[t % 8], 16)
                    fetched = ahead
                    add(s)
                def add_planes(g):
                    cols = slice(g * GI * D, (g + 1) * GI * D)
                    pool.wait_ge(part_in[g], 16 + 64 * (f + 1))
                    pool.tensor_tensor(out=PLANES[2][:, cols], in0=PLANES[2][:, cols], in1=PLANES[3][:, cols],
                                       op=ALU.add).then_inc(planes_added, 1)

                for g in range(EARLY, NSH):
                    if g >= NSH - 2:
                        add_planes(g - (NSH - 2))
                    shared_gates(g)
                for g in range(2, NG):
                    add_planes(g)
                if f == 0:
                    pool.wait_ge(group_ready, NG)
                    pool.sem_inc(vx_ready, PRIMED)

                    def block_diagonal(b, par):
                        pool.wait_ge(v_ready, b + 1)
                        pool.wait_ge(o_ps, PRIMED + b)
                        for c in range(NC):
                            pool.tensor_tensor(out=VX[:, :, :, c, :].rearrange("p q h f -> p (q h) f"),
                                               in0=VN[par].rearrange("p q h f -> p (q h) f"),
                                               in1=chm[:, c:c + 1].unsqueeze(2).broadcast_to([P, NQ * HEADS, E + 1]),
                                               op=ALU.mult).then_inc(vx_ready, 1)

                    with pool.Fori(0, B // 2) as i:
                        block_diagonal(2 * i, 0)
                        block_diagonal(2 * i + 1, 1)

        @block.scalar
        def _(act):
            act.wait_ge(ident_ready, 1)

            def norm(n, token_order, exponentials=None):
                def copies(j):
                    for g in (2 * j, 2 * j + 1):
                        act.wait_ge(xT_ps, n * NSH + g + 1)
                        if token_order:
                            dst = XT[:, :].rearrange("d (p i) -> d i p", i=NI)[:, 4 * g:4 * g + 4, :]
                            src = bank[g % 2][:, :].rearrange("d (i p) -> d i p", i=4)
                        else:
                            dst, src = XT[:, 512 * g:512 * g + 512], bank[g % 2][:, :]
                        act.activation(dst, src, ACT.Copy).then_inc(xT_sb, 1)

                def normalise(j):
                    act.wait_ge(scale_ready, NG * n + j + 1)
                    for i in range(GI * j, GI * j + GI):
                        ins = act.activation(A[:, i, :], X[:, i, :], ACT.Identity, bias=st[:, 1, i:i + 1],
                                             scale=st[:, 4, i:i + 1])
                    ins.then_inc(normed[j], 1)

                for j in range(NG + 1):
                    if j < NG:
                        act.wait_ge(stats_ready, NG * n + j + 1)
                        act.activation(st[:, 3, GI * j:GI * j + GI], mv[:, GI * j:GI * j + GI, 1], ACT.Sqrt,
                                       bias=eps[:, 0:1]).then_inc(std_ready, 1)
                    if 0 < j < NG:
                        normalise(j - 1)
                    if j >= 2:
                        if exponentials and j > 3:
                            exponentials(j - 4)
                        copies(j - 2)
                if exponentials:
                    exponentials(1)
                copies(NG - 1)

            def ffn(f):
                def exponentials(g):
                    act.wait_ge(shifted, NG * f + g + 1)
                    ex = EX[:, GI * g:GI * g + GI, :]
                    act.activation(ex, ex, ACT.Exp).then_inc(exp_done, 1)

                norm(2 * f, False, exponentials)
                for g in range(2, NG):
                    exponentials(g)

                def shared_copies(g):
                    SH, H3, HS = SHARED_BUFS[g >= EARLY]
                    for k in range(2):
                        n = (f * NSH + g) * 2 + k
                        b1, b3 = SHARED[k]
                        act.wait_ge(sh_ps, n + 1)
                        if n >= 2:
                            act.wait_ge(sh_gated, n - 1)
                        act.activation(SH[k], bank[b1][0:I, :], ACT.Silu).then_inc(sh_copied, 1)
                        act.activation(H3[k], bank[b3][0:I, :], ACT.Copy).then_inc(sh_copied, 1)

                def shared_add(g):
                    act.wait_ge(z_ps, f * NSH + g + 1)
                    act.activation(X[:, 4 * g:4 * g + 4, :].rearrange("p i d -> p (i d)"), bank[7][:, :], ACT.Copy,
                                   scale=0.5).then_inc(z_added, 1)

                def shared(first, last):
                    for g in range(first, last + 1):
                        if g < last:
                            shared_copies(g)
                        if g > first:
                            shared_add(g - 1)

                shared(0, EARLY)

                def copy_xbT(s):
                    act.wait_ge(xbT_ps, f * NS + s + 1)
                    if s >= 2:
                        act.wait_ge(h_ps, f * NS + s - 1)
                    act.activation(XBT[s % 2], bank[(0, 5)[s % 2]][:, 0:P], ACT.Copy).then_inc(xbT_sb, 1)

                def silu(s):
                    act.wait_ge(h_ps, f * NS + s + 1)
                    if s >= 2:
                        act.wait_ge(gated, f * NS + s - 1)
                    act.activation(SG[s % 2], bank[2 + s % 2][:, 0:I], ACT.Silu)\
                        .then_inc(silu_done, 1)

                def copy_gT(s):
                    act.wait_ge(gT_ps, f * NS + s + 1)
                    if s >= 2:
                        act.wait_ge(y_ps, f * NS + s - 1)
                    act.activation(GT[s % 2], bank[(1, 6)[s % 2]][0:I, 0:P], ACT.Copy).then_inc(gT_sb, 1)

                for s in range(NS + 3):
                    if s < NS:
                        copy_xbT(s)
                    if 1 <= s <= NS:
                        silu(s - 1)
                    if 2 <= s <= NS + 1:
                        copy_gT(s - 2)
                shared(EARLY, NSH)

            ffn(0)

            norm(1, True)
            act.wait_ge(xT_sb, 2 * NSH)
            act.wait_ge(small_in, 16 * N_SMALL)
            act.activation(bq[:, 2:3], bq[:, 2:3], ACT.Copy, scale=QS).then_inc(bq_scaled, 1)
            act.wait_ge(bq_scaled, 1)
            act.sem_inc(kn_sb, PRIMED)

            def slice_h(b):
                act.wait_ge(v_ps, PRIMED + b)
                act.activation(HTB, XT[:, bass.ds(b * L, L)], ACT.Copy).then_inc(hTb_sb, 1)

            def features(b):
                act.wait_ge(qT_ps, b + 1)
                act.wait_ge(q_ready, PRIMED + b)
                act.activation(EQ, bank[0][:, :], ACT.Exp, bias=bq[:, 2:3], scale=QS).then_inc(q_read, 1)
                act.activation(RQ, bank[0][:, :], ACT.Relu, bias=bq[:, 2:3], scale=QS).then_inc(q_read, 1)
                act.wait_ge(kT_ps, b + 1)
                act.wait_ge(k_ready, PRIMED + b)
                act.activation(EK, bank[1][:, :], ACT.Exp, bias=bq[:, 1:2]).then_inc(k_read, 1)
                act.activation(RK, bank[1][:, :], ACT.Relu, bias=bq[:, 1:2]).then_inc(k_read, 1)

            def split_q(b, par):
                act.wait_ge(q_ready, PRIMED + b + 1)
                act.wait_ge(sc_ps, PRIMED + 4 * b)
                for j in range(4):
                    act.activation(Q4[:, j, :], QT[par], ACT.Copy, scale=hm[:, j:j + 1]).then_inc(q4_ready, 1)

            def copy_kn(b):
                act.wait_ge(kn_ps, b + 1)
                act.wait_ge(kv_ps, PRIMED + NH * b)
                for c in range(NC):
                    act.activation(KN[:, c, :, :].rearrange("p q k -> p (q k)"), bank[3][:, :], ACT.Copy,
                                   scale=upto[:, c:c + 1]).then_inc(kn_sb, 1)

            def copy_anT(b):
                act.wait_ge(anT_ps, PRIMED + b + 1)
                act.wait_ge(pr_ps, PRIMED + b)
                act.activation(AT, bank[3][:, :], ACT.Copy).then_inc(anT_sb, 1)

            def step(b, par, first=False, last=False):
                if not last:
                    features(b + 1)
                    if not (isinstance(b, int) and b + 2 >= B):
                        slice_h(b + 2)
                if not first:
                    copy_anT(b - 1)
                if not last:
                    split_q(b + 1, 1 - par)
                    copy_kn(b + 1)

            slice_h(0)
            features(0)
            slice_h(1)
            split_q(0, 0)
            copy_kn(0)
            step(0, 0, first=True)
            with act.Fori(0, (B - 2) // 2 - 1) as i:
                step(2 * i + 1, 1)
                step(2 * i + 2, 0)
            step(B - 3, 1)
            step(B - 2, 0)
            step(B - 1, 1, last=True)
            copy_anT(B - 1)

            ffn(1)

        @block.tensor
        def _(pe):
            pe.wait_ge(ident_ready, 1)

            def xT(n, g):
                pe.wait_ge(normed[g // 2], n + 1)
                if g >= 2:
                    pe.wait_ge(xT_sb, n * NSH + g - 1)
                for i in range(4 * g, 4 * g + 4):
                    ins = pe.transpose(bank[g % 2][:, (i % 4) * P:(i % 4 + 1) * P], A[:, i, :], ident[:, :])
                ins.then_inc(xT_ps, 1)

            def ffn(f):
                def logits(g):
                    pe.wait_ge(xT_sb, 2 * f * NSH + 2 * g + 2)
                    for i in range(8 * g, 8 * g + 8):
                        ins = pe.matmul(bank[2 + g][:, (i % 8) * NE:(i % 8 + 1) * NE], XT[:, i * P:(i + 1) * P],
                                        gate_s[:, :], start=True, stop=True)
                    ins.then_inc(logits_ps, 1)

                for g in range(NG):
                    if g == 1:
                        pe.wait_ge(small_in, 16 * N_SMALL)
                    xT(2 * f, 2 * g)
                    xT(2 * f, 2 * g + 1)
                    if g:
                        logits(g - 1)
                logits(NG - 1)
                pe.wait_ge(const_done, 1)

                def shared_hidden(g, k):
                    n = (f * NSH + g) * 2 + k
                    if g == 0 and k == 1:
                        pe.wait_ge(shifted, NG * (f + 1))
                    if g == EARLY:
                        pe.wait_ge(y_sb, (f + 1) * NS)
                    if g:
                        pe.wait_ge(sh_copied, 2 * (n - 1))
                    for w, bk in zip((ws1s, ws3s), SHARED[k]):
                        ins = pe.matmul(bank[bk][0:I, :], w[:, k * I:(k + 1) * I], XT[:, 512 * g:512 * g + 512],
                                        start=True, stop=True)
                    ins.then_inc(sh_ps, 1)

                def shared_out(g):
                    n = f * NSH + g
                    if n:
                        pe.wait_ge(z_added, n)
                    pe.matmul(bank[7][:, :], twice[:, :], X[:, 4 * g:4 * g + 4, :].rearrange("p i d -> p (i d)"),
                              start=True, stop=False, skip_group_check=True)
                    pe.wait_ge(sh_gated, 2 * n + 2)
                    for i in range(4):
                        for k in range(2):
                            ins = pe.matmul(bank[7][:, i * D:(i + 1) * D], SHARED_BUFS[g >= EARLY][2][g % 2][k][:, i * P:(i + 1) * P], ws2s[:, k, :],
                                            start=False, stop=(k == 1), skip_group_check=True)
                    ins.then_inc(z_ps, 1)

                def base():
                    pe.wait_ge(totals, f + 1)
                    pe.matmul(bank[6][:, 0:NE], before[:, :], st2[:, 1, :], start=True, stop=True).then_inc(base_ps, 1)

                def look_up():
                    for s in range(NS):
                        if s == 2 * PER:
                            pe.wait_ge(sh_copied, 4 * (f * NSH + EARLY))
                        if s % (NS // NQT) == 0:
                            pe.wait_ge(table_ready, NQT * f + s // (NS // NQT) + 1)
                            pe.wait_ge(counts_ready, NQT * f + s // (NS // NQT) + 1)
                        for k in range(2):
                            e = 2 * s + k
                            ins = pe.matmul(bank[2 + s // PER][CAP * k:CAP * k + CAP, (s % PER) * RW:(s % PER + 1) * RW],
                                            OH[:, e, :], R[:, e, :], start=True, stop=True)
                        if s % PER == PER - 1 or s == NS - 1:
                            ins.then_inc(look_ps, 1)
                            if s // PER == 0:
                                shared_hidden(EARLY - 1, 1)
                            elif s // PER < 3:
                                shared_out(EARLY - 3 + s // PER)

                for g in range(EARLY):
                    shared_hidden(g, 0)
                    if g < EARLY - 1:
                        shared_hidden(g, 1)
                        if g == BASE_AFTER:
                            base()
                        if g:
                            shared_out(g - 1)
                look_up()
                pe.wait_ge(z_added, f * NSH + EARLY)
                pe.wait_ge(w_in, 48 + 16 * f)

                def looked_up(bk):
                    pe.wait_ge(slots_ready, NB * f + bk - 1)

                def xb_turn(s):
                    if s == 1:
                        looked_up(5)
                    pe.wait_ge(gathered[s % 8], 16 * (f * (NS // 8) + s // 8 + 1))
                    if s >= 2:
                        pe.wait_ge(xbT_sb, f * NS + s - 1)
                    pe.transpose(bank[(0, 5)[s % 2]][:, 0:P], A[:, s, :], ident[:, :]).then_inc(xbT_ps, 1)

                def hidden(s):
                    pe.wait_ge(xbT_sb, f * NS + s + 1)
                    if s < 2:
                        looked_up(2 + s)
                    if s >= 2:
                        pe.wait_ge(gated, f * NS + s - 1)
                    for w, off in ((w1s, 0), (w3s, I)):
                        for k in range(2):
                            ins = pe.matmul(bank[2 + s % 2][CAP * k:CAP * k + CAP, off:off + I], XBT[s % 2][:, CAP * k:CAP * k + CAP],
                                            w[:, 2 * s + k, :], start=True, stop=True)
                    ins.then_inc(h_ps, 1)

                def g_turn(s):
                    pe.wait_ge(gated, f * NS + s + 1)
                    if s == 1:
                        looked_up(6)
                    if s >= 2:
                        pe.wait_ge(gT_sb, f * NS + s - 1)
                    pe.transpose(bank[(1, 6)[s % 2]][0:I, 0:P], GA[s % 2], ident[:, :]).then_inc(gT_ps, 1)

                def expert_out(s):
                    pe.wait_ge(gT_sb, f * NS + s + 1)
                    if s >= 2:
                        pe.wait_ge(y_sb, f * NS + s - 1)
                    for k in range(2):
                        ins = pe.matmul(bank[(4, 7)[s % 2]][CAP * k:CAP * k + CAP, 0:D], GT[s % 2][:, CAP * k:CAP * k + CAP],
                                        w2s[:, 2 * s + k, :], start=True, stop=True)
                    ins.then_inc(y_ps, 1)

                for s in range(NS + 3):
                    if s < NS:
                        xb_turn(s)
                    if 1 <= s <= NS:
                        hidden(s - 1)
                    if 2 <= s <= NS + 1:
                        g_turn(s - 2)
                    if s >= 3:
                        expert_out(s - 3)
                for g in range(EARLY, NSH):
                    for k in range(2):
                        shared_hidden(g, k)
                    if g > EARLY:
                        shared_out(g - 1)
                shared_out(NSH - 1)

            ffn(0)

            for g in range(NSH):
                xT(1, g)
            pe.wait_ge(xT_sb, 2 * NSH)
            for s in (v_ps, sc_ps, kv_ps, pr_ps, o_ps, anT_ps):
                pe.sem_inc(s, PRIMED)

            def project(b):
                pe.wait_ge(hTb_sb, b + 1)
                if not (isinstance(b, int) and b == 0):
                    pe.wait_ge(kv_sb, PRIMED + NH * (b - 1))
                    pe.wait_ge(q_read, 2 * b)
                    pe.wait_ge(v_ready, b)
                    pe.wait_ge(k_read, 2 * b)
                pe.matmul(bank[0][:, :], wqkv[:, 0:D], HTB, start=True, stop=True).then_inc(qT_ps, 1)
                pe.matmul(bank[1][:, :], wqkv[:, D:2 * D], HTB, start=True, stop=True).then_inc(kT_ps, 1)
                for q in range(NQ):
                    ins = pe.matmul(bank[2][:, q * D:(q + 1) * D], HTB[:, q * P:(q + 1) * P], wqkv[:, 2 * D:3 * D],
                                    start=True, stop=True)
                ins.then_inc(v_ps, 1)

            def turn_k(b):
                if not (isinstance(b, int) and b == 0):
                    pe.wait_ge(oo_ready, PRIMED + b - 1)
                pe.wait_ge(k_ready, PRIMED + b + 1)
                for q in range(NQ):
                    ins = pe.transpose(bank[3][:, q * P:(q + 1) * P], KT[:, q * P:(q + 1) * P], ident[:, :])
                ins.then_inc(kn_ps, 1)

            def turn_out(b):
                if not (isinstance(b, int) and b == B - 1):
                    pe.wait_ge(kn_sb, PRIMED + NC * (b + 2))
                pe.wait_ge(an_ready, 2 * (b + 1))
                for c in range(NC):
                    ins = pe.transpose(bank[3][:, c * P:(c + 1) * P], AN[:, c, :], ident[:, :])
                ins.then_inc(anT_ps, 1)

            def project_out(b):
                pe.wait_ge(anT_sb, b + 1)
                for c in range(NC):
                    ins = pe.matmul(bank[3][:, c * D:(c + 1) * D], AT[:, c * P:(c + 1) * P], wout[:, :],
                                    start=True, stop=True)
                ins.then_inc(pr_ps, 1)

            def step(b, par, first=False, last=False):
                if not last:
                    project(b + 1)
                pe.wait_ge(q4_ready, 4 * b + 4)
                pe.wait_ge(k_ready, PRIMED + b + 1)
                if not first:
                    turn_out(b - 1)
                for g in range(4):
                    rows = slice(32 * g, 32 * g + 32)
                    for q in range(NQ):
                        for c in range(NC):
                            t0 = q * P + c * CHUNK
                            ins = pe.matmul(bank[4 + g][CHUNK * c:CHUNK * c + CHUNK, q * P:(q + 1) * P]
                                            .rearrange("p (j t) -> p j t", j=4),
                                            KT[rows, t0:t0 + CHUNK], Q4[rows, :, t0:t0 + CHUNK],
                                            start=True, stop=True)
                    ins.then_inc(sc_ps, 1)
                    if g == 1:
                        pe.wait_ge(kn_sb, PRIMED + NC * (b + 1))
                        if last:
                            pe.wait_ge(v_ready, b + 1)
                        else:
                            pe.wait_ge(v_ready, b + 2)
                            pe.wait_ge(q_read, 2 * (b + 2))
                            pe.wait_ge(k_read, 2 * (b + 2))
                    for m in AFTER[g]:
                        q = m // 2
                        if m >= len(STATES):
                            pe.wait_ge(kv_sb, PRIMED + NH * b + m + 1 - len(STATES))
                        for k in range(1 if m == NH - 1 else 2):
                            ins = pe.matmul(bank[STATES[m % len(STATES)]][:, k * VW:(k + 1) * VW], KN[:, 2 * (m % 2) + k, q, :],
                                            VN[par][:, q, :, :].rearrange("p h f -> p (h f)"), start=True, stop=True)
                        ins.then_inc(kv_ps, 1)
                if not first:
                    project_out(b - 1)
                pe.wait_ge(vx_ready, PRIMED + NC * (b + 1))
                pe.wait_ge(sc_sb, 4 * b + 4)
                for h in range(HEADS):
                    ob = bank[4 + h // 8][:, 0:NC * HV].rearrange("p (c h f) -> p c h f", c=NC, h=8)
                    for q in range(NQ):
                        o = (h // 4) * L + q * P + (h % 4) * CHUNK
                        pe.matmul(ob[32 * q:32 * q + 32, :, h % 8, :], PR[:, o:o + CHUNK],
                                  VX[:, q, h, :, :], start=(h % 8 == 0), stop=False, skip_group_check=True)
                pe.wait_ge(kv_sb, PRIMED + NH * (b + 1))
                pe.wait_ge(sb_ready, (NQ - 1) * (b + 1))
                for half in range(2):
                    for c in range(NC):
                        for q in range(NQ):
                            if q + c == 0:
                                continue
                            t0 = q * P + c * CHUNK
                            before_c = SW[:, q, c - 1, :] if c else SW[:, q - 1, NC - 1, :]
                            ins = pe.matmul(bank[4 + half][32 * q:32 * q + 32, c * HV:(c + 1) * HV], QT[par][:, t0:t0 + CHUNK],
                                            before_c[:, half * HV:(half + 1) * HV], start=False, stop=True, skip_group_check=True)
                ins.then_inc(o_ps, 1)
                if not last:
                    turn_k(b + 1)

            project(0)
            turn_k(0)
            step(0, 0, first=True)
            with pe.Fori(0, (B - 2) // 2) as i:
                step(2 * i + 1, 1)
                step(2 * i + 2, 0)
            step(B - 1, 1, last=True)
            turn_out(B - 1)
            project_out(B - 1)

            ffn(1)

        @block.vector
        def _(dve):
            steps = [0]

            def then(ins):
                steps[0] += 1
                ins.then_inc(dve_step, 1)
                dve.wait_ge(dve_step, steps[0])

            def over(v, n):
                return v.unsqueeze(2).broadcast_to([P, v.shape[1], n])

            dve.memset(zeros[:, :], 0.0).then_inc(zero_set, 1)
            dve.memset(top8[:, :, :], 0.0)

            def norm(n):
                def update(g):
                    xg = X[:, GI * g:GI * g + GI, :].rearrange("p i d -> p (i d)")
                    cols = slice(g * GI * D, (g + 1) * GI * D)
                    if n == 0:
                        dve.wait_ge(part_in[g], 16)
                        return
                    if n == 2:
                        dve.wait_ge(attn_in[g], 16 * B)
                        then(dve.tensor_tensor(xg, xg, PL[:, cols], ALU.add))
                        return
                    dve.wait_ge(z_added, NSH * (n // 2) + 2 * g + 2)
                    dve.wait_ge(part_in[g], 16 + 64 * (1 + n // 2))
                    for buf in PLANES[0:3]:
                        if buf is PLANES[2]:
                            dve.wait_ge(planes_added, NG * (n // 2) + g + 1)
                        then(dve.tensor_tensor(xg, xg, buf[:, cols], ALU.add))
                    dve.memset(st[:, 0, 0:1], 0.0).then_inc(group_ready, 1)

                def stats(g):
                    for i in range(GI * g, GI * g + GI):
                        ins = dve.bn_stats(bn[:, i, :], X[:, i, :])
                    then(ins)
                    for i in range(GI * g, GI * g + GI):
                        ins = dve.bn_aggr(mv[:, i, :], bn[:, i, :])
                    ins.then_inc(stats_ready, 1)

                def scales(g):
                    dve.wait_ge(std_ready, NG * n + g + 1)
                    cols = slice(GI * g, GI * g + GI)
                    then(dve.reciprocal(st[:, 4, cols], st[:, 3, cols]))
                    dve.scalar_tensor_tensor(st[:, 1, cols], mv[:, cols, 0], -1.0, st[:, 4, cols], ALU.mult, ALU.mult)\
                        .then_inc(scale_ready, 1)

                for g in range(NG):
                    update(g)
                    if n < 3:
                        stats(g)
                        if g:
                            scales(g - 1)
                if n < 3:
                    g = NG - 1
                    scales(g)
                    for i in range(GI * g, GI * g + GI):
                        ins = dve.tensor_scalar(A[:, i, :], X[:, i, :], mv[:, i, 0:1], st[:, 4, i:i + 1],
                                                ALU.subtract, ALU.mult)
                    ins.then_inc(normed[g], 1)

            def ffn(f):
                norm(2 * f)
                if f == 0:
                    dve.wait_ge(const_done, 1)
                    dve.wait_ge(small_in, 16 * N_SMALL)
                def shift(g):
                    dve.wait_ge(logits_ps, NG * f + g + 1)
                    lg = bank[2 + g][:, :].rearrange("p (i e) -> p i e", i=GI)
                    tiles = slice(GI * g, GI * g + GI)
                    then(dve.tensor_reduce(st[:, 5, tiles], lg, AX, ALU.max))
                    dve.tensor_tensor(EX[:, tiles, :], lg, over(st[:, 5, tiles], NE), ALU.subtract).then_inc(shifted, 1)

                def total(g):
                    dve.wait_ge(exp_done, NG * f + g + 1)
                    tiles = slice(GI * g, GI * g + GI)
                    then(dve.tensor_reduce(st[:, 6, tiles], EX[:, tiles, :], AX, ALU.add))
                    dve.reciprocal(st[:, 7, tiles], st[:, 6, tiles]).then_inc(recip_ready, 1)

                def top(g):
                    dve.wait_ge(biased, NG * f + g + 1)
                    tiles = slice(GI * g, GI * g + GI)
                    for i in range(GI * g, GI * g + GI):
                        ins = dve.max(top8[:, i, :], BI[:, i, 0:NE])
                    then(ins)
                    dve.memset(top8[:, tiles, TOPK:TOPK + 1], -1e30)
                    then(dve.memset(top8[:, tiles, TOPK + 1:TOPK + 2], -2e30))
                    for i in range(GI * g, GI * g + GI):
                        ins = dve.match_replace(RP[:, i, :], top8[:, i, :], BI[:, i, :], -3e30)
                    return ins

                dve.memset(BI[:, :, NE:NE + 1], -1e30)
                dve.memset(BI[:, :, NE + 1:NE + 2], -2e30)
                shift(0)
                shift(1)
                total(0)
                shift(2)
                total(1)
                top(0)
                shift(3)
                total(2)
                top(1)
                total(3)
                top(2)
                then(top(3))
                then(dve.tensor_tensor(M.rearrange("p e i -> p i e"), RP[:, :, 0:NE], BI[:, :, 0:NE], ALU.not_equal))
                dve.wait_ge(rows_out, 16 * NG * (f + 1))
                dve.wait_ge(xT_ps, (2 * f + 1) * NSH)
                then(dve.tensor_tensor_scan(A_flat[:, 0:NE * NI], Eb[:, :], Eb[:, :], 0.0, ALU.add, ALU.max))
                dve.memset(st2[:, 0, 0:1], 0.0)
                then(dve.tensor_copy(st2[:, 0, 1:NE], CUM[:, 0:NE - 1, NI - 1]))
                dve.tensor_tensor(st2[:, 1, :], CUM[:, :, NI - 1], st2[:, 0, :], ALU.subtract).then_inc(totals, 1)
                dve.wait_ge(base_ps, f + 1)
                then(dve.tensor_copy(st2[:, 2, :], bank[6][:, 0:NE]))
                then(dve.tensor_tensor(st2[:, 3, :], st2[:, 2, :], st2[:, 1, :], ALU.add))
                dve.tensor_tensor(st2[:, 4, :], st2[:, 2, :], st2[:, 0, :], ALU.subtract).then_inc(base_ready, 1)
                dve.tensor_scalar(R[:, :, 2 * NI], st2[:, 0, :], 0.0, tok0[:, 0:1], ALU.mult, ALU.add)
                then(dve.tensor_scalar(bnd[:, :, :], st2[:, 2:4, :], float(CAP), None, ALU.min))
                def one_hot(h):
                    ex = slice(HE * h, HE * h + HE)
                    c_h = slot_ce[:, :, ex]
                    ge, lt = GL[h % 2]
                    if h >= 2:
                        dve.wait_ge(table_ready, NQT * f + h - 1)
                    dve.tensor_tensor(ge, c_h, bnd[:, 0:1, ex].broadcast_to([P, CAP, HE]), ALU.is_ge)
                    then(dve.tensor_tensor(lt, c_h, bnd[:, 1:2, ex].broadcast_to([P, CAP, HE]), ALU.is_lt))
                    dve.tensor_tensor(OH[:, ex, :].rearrange("p e c -> p c e"), ge, lt, ALU.mult).then_inc(table_ready, 1)

                def slots(b):
                    ss = slice(PER * b, min(PER * b + PER, NS))
                    n = ss.stop - ss.start
                    dve.wait_ge(look_ps, NB * f + b + 1)
                    bk = bank[2 + b][:, 0:n * RW].rearrange("p (s r) -> p s r", s=n)
                    then(dve.tensor_scalar(LE[:, ss, :], bk[:, :, 0:NI], c_of_p[:, 0:1], None, ALU.is_le))
                    then(dve.tensor_reduce(sl[:, 0, ss], LE[:, ss, :], AX, ALU.add))
                    dve.scalar_tensor_tensor(sl[:, 1, ss], sl[:, 0, ss], -NONE, bk[:, :, 2 * NI], ALU.add, ALU.add)
                    then(dve.tensor_tensor(LE[:, ss, :], col_i[:, :].unsqueeze(1).broadcast_to([P, n, NI]),
                                           over(sl[:, 0, ss], NI), ALU.is_equal))
                    dve.tensor_copy(tok_i[:, ss], sl[:, 1, ss])
                    dve.tensor_tensor(put_i[:, ss], sl[:, 1, ss], plane0[:, ss], ALU.add).then_inc(tokens_ready, 1)
                    then(dve.tensor_tensor(LE[:, ss, :], LE[:, ss, :], bk[:, :, NI:2 * NI], ALU.mult))
                    dve.tensor_reduce(sl[:, 2, ss], LE[:, ss, :], AX, ALU.add).then_inc(slots_ready, 1)

                one_hot(0)
                for h in range(1, NQT):
                    one_hot(h)
                    slots(h - 1)
                for b in range(NQT - 1, NB):
                    slots(b)
                dve.wait_ge(slots_ready, NB * (f + 1))

                def gate(s):
                    dve.wait_ge(silu_done, f * NS + s + 1)
                    if s >= 2:
                        dve.wait_ge(gT_ps, f * NS + s - 1)
                    dve.tensor_tensor(GA[s % 2], SG[s % 2], bank[2 + s % 2][:, I:2 * I], ALU.mult).then_inc(gated, 1)

                def weigh(s):
                    dve.wait_ge(y_ps, f * NS + s + 1)
                    dve.tensor_scalar(Y[:, s, :], bank[(4, 7)[s % 2]][:, 0:D], sl[:, 2, s:s + 1], 0.5,
                                      ALU.mult, ALU.mult).then_inc(y_sb, 1)

                for s in range(NS + 3):
                    if 1 <= s <= NS:
                        gate(s - 1)
                    if s >= 3:
                        weigh(s - 3)
            ffn(0)

            norm(1)
            for v in VN:
                then(dve.memset(v, 1.0))
            for s in (q_ready, k_ready, kv_sb, oo_ready):
                dve.sem_inc(s, PRIMED)

            def feature(b, k, e, r, dst, last_readers):
                dve.wait_ge((q_read, k_read)[k], 2 * (b + 1))
                dve.tensor_scalar(e, e, 1.0, FEAT_EPS, ALU.min, ALU.add).then_inc(phi_step, 1)
                dve.wait_ge(phi_step, 2 * b + k + 1)
                dve.wait_ge(*last_readers)
                dve.tensor_tensor(dst, e, r, ALU.add).then_inc((q_ready, k_ready)[k], 1)

            def value(b, par):
                dve.wait_ge(v_ps, PRIMED + b + 1)
                if not (isinstance(b, int) and b < 2):
                    dve.wait_ge(vx_ready, PRIMED + NC * (b - 1))
                    dve.wait_ge(kv_ps, PRIMED + NH * (b - 1))
                dve.tensor_tensor(VN[par][:, :, :, 0:E],
                                  bank[2][:, :].rearrange("p (q h f) -> p q h f", q=NQ, h=HEADS),
                                  bv[:, :].rearrange("p (h f) -> p h f", h=HEADS).unsqueeze(1)
                                  .broadcast_to([P, NQ, HEADS, E]), ALU.add).then_inc(v_ready, 1)

            def q_feature(b, par):
                n = PRIMED if isinstance(b, int) and b < 2 else PRIMED + b - 1
                feature(b, 0, EQ, RQ, QT[par], (o_ps, n))

            def k_feature(b):
                feature(b, 1, EK, RK, KT, (sc_ps, PRIMED + 4 * b))

            def project_bias(b):
                dve.wait_ge(pr_ps, PRIMED + b + 1)
                dve.wait_ge(oo_stored, PRIMED + b)
                dve.tensor_tensor(OO.rearrange("p (c d) -> p c d", c=NC),
                                  bank[3][:, :].rearrange("p (c d) -> p c d", c=NC),
                                  bo[:, :].unsqueeze(1).broadcast_to([P, NC, D]), ALU.add).then_inc(oo_ready, 1)

            def step(b, par, first=False, last=False):
                if not last:
                    value(b + 1, 1 - par)
                    q_feature(b + 1, 1 - par)
                for g in range(4):
                    dve.wait_ge(sc_ps, PRIMED + 4 * b + g + 1)
                    if g == 0:
                        dve.wait_ge(o_ps, PRIMED + b)
                    dve.tensor_tensor(PR[:, g * L:(g + 1) * L].rearrange("p (n t) -> p n t", t=CHUNK),
                                      bank[4 + g][:, :].rearrange("p (n t) -> p n t", t=CHUNK),
                                      causal[:, :].unsqueeze(1).broadcast_to([P, L // CHUNK, CHUNK]),
                                      ALU.mult).then_inc(sc_sb, 1)
                    for m in AFTER[g]:
                        q = m // 2
                        n = 1 if m == NH - 1 else 2
                        dve.wait_ge(kv_ps, PRIMED + NH * b + m + 1)
                        dve.tensor_tensor(SW[:, q, 2 * (m % 2):2 * (m % 2) + n, :],
                                          bank[STATES[m % len(STATES)]][:, 0:n * VW].rearrange("p (c v) -> p c v", c=n),
                                          own[:, :].unsqueeze(1).broadcast_to([P, n, VW]), ALU.mult).then_inc(kv_sb, 1)
                        if q and m % 2:
                            n = NC if q < NQ - 1 else NC - 1
                            dve.wait_ge(kv_sb, PRIMED + NH * b + 2 * q + 2)
                            if q > 1:
                                dve.wait_ge(sb_ready, (NQ - 1) * b + q - 1)
                            dve.tensor_tensor(SW[:, q, 0:n, :], SW[:, q, 0:n, :],
                                              SW[:, q - 1, NC - 1:NC, :].broadcast_to([P, n, VW]), ALU.add).then_inc(sb_ready, 1)
                if not last:
                    k_feature(b + 1)
                if not first:
                    project_bias(b - 1)
                dve.wait_ge(o_ps, PRIMED + b + 1)
                if not first:
                    dve.wait_ge(anT_ps, PRIMED + b)
                for k in range(2):
                    ob = bank[4 + k][:, 0:NC * HV].rearrange("p (n f) -> p n f", f=E + 1)
                    den = top8[:, 8 * k:8 * k + 4, :].rearrange("p a b -> p (a b)")
                    rec = top8[:, 8 * k + 4:8 * k + 8, :].rearrange("p a b -> p (a b)")
                    dve.tensor_scalar(den, ob[:, :, E], DEN_EPS, None, ALU.add).then_inc(o_step, 1)
                    dve.wait_ge(o_step, 4 * b + 2 * k + 1)
                    dve.reciprocal(rec, den).then_inc(o_step, 1)
                    dve.wait_ge(o_step, 4 * b + 2 * k + 2)
                    dve.tensor_tensor(AN[:, :, k * 8 * E:(k + 1) * 8 * E].rearrange("p c (h f) -> p c h f", h=8),
                                      bank[4 + k][:, 0:NC * HV].rearrange("p (c h f) -> p c h f", c=NC, h=8)[:, :, :, 0:E],
                                      rec.rearrange("p (c h) -> p c h", c=NC).unsqueeze(3)
                                      .broadcast_to([P, NC, 8, E]), ALU.mult).then_inc(an_ready, 1)

            value(0, 0)
            q_feature(0, 0)
            k_feature(0)
            step(0, 0, first=True)
            with dve.Fori(0, (B - 2) // 2) as i:
                step(2 * i + 1, 1)
                step(2 * i + 2, 0)
            step(B - 1, 1, last=True)
            project_bias(B - 1)

            ffn(1)
            norm(3)


def kernel(**inputs):
    import numpy as _np
    import concourse.bacc as _bacc
    from concourse import mybir as _mybir
    from concourse.bass_utils import run_bass_kernel_spmd as _run

    a = {k: _np.asarray(v) for k, v in inputs.items()}
    inner = a["L0_ffn_w1"].shape[1]
    laid = {
        "x": a["L0_attn_x"],
        "w_qkv": a["L0_attn_W_qkv"],
        "b_qkv": a["L0_attn_b_qkv"],
        "w_out": a["L0_attn_W_out"],
        "b_out": a["L0_attn_b_out"],
        "gate_wT": a["L0_ffn_gate_w"].T,
        "gate_b": a["L0_ffn_gate_b"],
        "w1T": a["L0_ffn_w1"].transpose(2, 0, 1),
        "w2T": a["L0_ffn_w2"].transpose(2, 0, 1),
        "w3T": a["L0_ffn_w3"].transpose(2, 0, 1),
        "ws1T": a["L0_ffn_ws1"].T,
        "ws2T": a["L0_ffn_ws2"].T.reshape(2, inner, -1).transpose(1, 0, 2),
        "ws3T": a["L0_ffn_ws3"].T,
    }
    nc = _bacc.Bacc("TRN2", target_bir_lowering=False, num_devices=1)
    arrays, args = {}, []
    for name, v in laid.items():
        v = _np.ascontiguousarray(v)
        arrays[f"in_{name}"] = v
        args.append(nc.dram_tensor(f"in_{name}", v.shape, _mybir.dt.from_np(v.dtype), kind="ExternalInput").ap())
    out = nc.dram_tensor("out_x", laid["x"].shape, _mybir.dt.from_np(laid["x"].dtype), kind="ExternalOutput").ap()
    macaron_kernel(nc, *args, out)
    r = _run(nc, [arrays], core_ids=[0])
    return r.results[0]["out_x"]
```
